# Optimizing a Trainium2 kernel written in Bass

```python
import numpy as np
import jax
import jax.numpy as jnp

def _softmax(x, axis=-1):
    return jax.nn.softmax(x, axis=axis)

def _gelu(x):
    return jax.nn.gelu(x, approximate=True)

def _silu(x):
    return jax.nn.silu(x)

def _sigmoid(x):
    return jax.nn.sigmoid(x)

def _layernorm(x, axis=-1, eps=1e-05):
    m = jnp.mean(x, axis=axis, keepdims=True)
    v = jnp.var(x, axis=axis, keepdims=True)
    return (x - m) / jnp.sqrt(v + eps)

def _scatter_add(tgt, idx, src, axis=0):
    return tgt.at[idx].add(src)

def _segment_sum(src, seg, n):
    return jax.ops.segment_sum(src, seg, n)
kernel_name = 'mk_prb_d1_jaxref_r8_9901a1'

def setup_inputs(seed: int=0):
    np.random.seed(seed)
    _w = jnp.asarray

    def _L0_attn_setup():
        import jax, jax.numpy as jnp
        import numpy as np
        N_HEAD = 16
        N_KV = 4
        N_EMBD = 256
        HEAD_DIM = N_EMBD // N_HEAD
        GROUP = N_HEAD // N_KV
        key = jax.random.key(seed)
        ks = jax.random.split(key, 5)
        B, S = (2, 256)
        scale = 0.02
        return {'x': jax.random.normal(ks[0], (B, S, N_EMBD), dtype=jnp.float32), 'Wq': jax.random.normal(ks[1], (N_EMBD, N_EMBD), dtype=jnp.float32) * scale, 'Wk': jax.random.normal(ks[2], (N_EMBD, N_EMBD // GROUP), dtype=jnp.float32) * scale, 'Wv': jax.random.normal(ks[3], (N_EMBD, N_EMBD // GROUP), dtype=jnp.float32) * scale, 'Wo': jax.random.normal(ks[4], (N_EMBD, N_EMBD), dtype=jnp.float32) * scale}
    _L0_attn_in = _L0_attn_setup()

    def _L0_ffn_setup():
        import jax, jax.numpy as jnp
        import numpy as np
        HIDDEN = 256
        INTER = 1024
        SCALE = 64.0

        def fwht(x):
            orig_shape = x.shape
            n = orig_shape[-1]
            x = x.reshape(-1, n)
            h = 1
            while h < n:
                x = x.reshape(-1, n // (2 * h), 2, h)
                a, b = (x[:, :, 0, :], x[:, :, 1, :])
                x = jnp.stack([a + b, a - b], axis=2).reshape(-1, n)
                h *= 2
            return (x / jnp.sqrt(jnp.asarray(n, x.dtype))).reshape(orig_shape)
        key = jax.random.key(seed)
        ks = jax.random.split(key, 8)
        inp = jax.random.normal(ks[0], (4, 256, HIDDEN), dtype=jnp.float32)
        SU_ug = jnp.where(jax.random.bernoulli(ks[1], 0.5, (HIDDEN,)), 1.0, -1.0).astype(jnp.float32)
        SU_dp = jnp.where(jax.random.bernoulli(ks[2], 0.5, (INTER,)), 1.0, -1.0).astype(jnp.float32)
        Wscale_ug = jax.random.uniform(ks[3], (2 * INTER,), jnp.float32, 0.5, 1.5)
        Wscale_dp = jax.random.uniform(ks[4], (HIDDEN,), jnp.float32, 0.5, 1.5)
        W_up = jax.random.normal(ks[5], (INTER, HIDDEN), dtype=jnp.float32) * 0.02
        W_gate = jax.random.normal(ks[6], (INTER, HIDDEN), dtype=jnp.float32) * 0.02
        W_down = jax.random.normal(ks[7], (HIDDEN, INTER), dtype=jnp.float32) * 0.02
        return {'input': inp, 'SU_ug': SU_ug, 'SU_dp': SU_dp, 'Wscale_ug': Wscale_ug, 'Wscale_dp': Wscale_dp, 'W_up': W_up, 'W_gate': W_gate, 'W_down': W_down}
    _L0_ffn_in = _L0_ffn_setup()
    _d = {'L0_attn_x': _L0_attn_in['x'], 'L0_attn_Wq': _L0_attn_in['Wq'], 'L0_attn_Wk': _L0_attn_in['Wk'], 'L0_attn_Wv': _L0_attn_in['Wv'], 'L0_attn_Wo': _L0_attn_in['Wo'], 'L0_ffn_SU_ug': _L0_ffn_in['SU_ug'], 'L0_ffn_SU_dp': _L0_ffn_in['SU_dp'], 'L0_ffn_Wscale_ug': _L0_ffn_in['Wscale_ug'], 'L0_ffn_Wscale_dp': _L0_ffn_in['Wscale_dp'], 'L0_ffn_W_up': _L0_ffn_in['W_up'], 'L0_ffn_W_gate': _L0_ffn_in['W_gate'], 'L0_ffn_W_down': _L0_ffn_in['W_down']}
    _x0 = _d['L0_attn_x']
    _d['L0_attn_x'] = jax.random.normal(jax.random.fold_in(jax.random.key(seed), 1), (2, 512, 256), dtype=_x0.dtype)
    del _x0
    return _d

def reference(L0_attn_x, L0_attn_Wq, L0_attn_Wk, L0_attn_Wv, L0_attn_Wo, L0_ffn_SU_ug, L0_ffn_SU_dp, L0_ffn_Wscale_ug, L0_ffn_Wscale_dp, L0_ffn_W_up, L0_ffn_W_gate, L0_ffn_W_down):

    def _L0_attn_ref(x, Wq, Wk, Wv, Wo):
        import jax, jax.numpy as jnp
        import numpy as np
        N_HEAD = 16
        N_KV = 4
        N_EMBD = 256
        HEAD_DIM = N_EMBD // N_HEAD
        GROUP = N_HEAD // N_KV
        B, S, _ = x.shape
        scale = HEAD_DIM ** (-0.5)
        q = (x @ Wq).reshape(B, S, N_KV, GROUP, HEAD_DIM)
        k = (x @ Wk).reshape(B, S, N_KV, HEAD_DIM)
        v = (x @ Wv).reshape(B, S, N_KV, HEAD_DIM)
        scores = jnp.einsum('bqkgd,bskd->bkgqs', q, k) * scale
        causal = jnp.triu(jnp.ones((S, S), dtype=bool), k=1)
        scores = jnp.where(causal, jnp.finfo(scores.dtype).min, scores)
        attn = jax.nn.softmax(scores, axis=-1)
        out = jnp.einsum('bkgqs,bskd->bqkgd', attn, v)
        out = out.reshape(B, S, N_EMBD)
        return out @ Wo

    def _L0_ffn_ref(input, SU_ug, SU_dp, Wscale_ug, Wscale_dp, W_up, W_gate, W_down):
        import jax, jax.numpy as jnp
        import numpy as np
        HIDDEN = 256
        INTER = 1024
        SCALE = 64.0

        def fwht(x):
            orig_shape = x.shape
            n = orig_shape[-1]
            x = x.reshape(-1, n)
            h = 1
            while h < n:
                x = x.reshape(-1, n // (2 * h), 2, h)
                a, b = (x[:, :, 0, :], x[:, :, 1, :])
                x = jnp.stack([a + b, a - b], axis=2).reshape(-1, n)
                h *= 2
            return (x / jnp.sqrt(jnp.asarray(n, x.dtype))).reshape(orig_shape)
        n = SU_ug.shape[0]
        x = input.reshape(-1, n)
        x = fwht(x * SU_ug) / SCALE
        x_up = x @ W_up.T * (Wscale_ug[:INTER] * SCALE)
        x_gate = x @ W_gate.T * (Wscale_ug[INTER:] * SCALE)
        x = jax.nn.silu(x_gate) * x_up
        x = fwht(x * SU_dp) / SCALE
        x = x @ W_down.T * (Wscale_dp * SCALE)
        return x.reshape(input.shape)
    x = L0_attn_x
    xn = _layernorm(x, axis=-1)
    x = x + _L0_attn_ref(xn, L0_attn_Wq, L0_attn_Wk, L0_attn_Wv, L0_attn_Wo) + _L0_ffn_ref(xn, L0_ffn_SU_ug, L0_ffn_SU_dp, L0_ffn_Wscale_ug, L0_ffn_Wscale_dp, L0_ffn_W_up, L0_ffn_W_gate, L0_ffn_W_down)
    return x

_drawn_inputs = setup_inputs


def setup_inputs(seed=0):
    import zlib

    import numpy as np

    out = dict(_drawn_inputs(seed))
    spreads = {}
    factors = {'L0_attn_Wq': 8.0,
     'L0_attn_Wk': 8.0,
     'L0_attn_Wv': 4.495,
     'L0_attn_Wo': 4.691,
     'L0_ffn_Wscale_ug': 3.96,
     'L0_ffn_Wscale_dp': 5.51}
    for name, (base, spread) in spreads.items():
        noise = np.random.default_rng([zlib.crc32(name.encode()), seed]).standard_normal(out[name].shape)
        drawn = base * np.exp(spread * noise) if base else spread * noise
        out[name] = jnp.asarray(drawn.astype(out[name].dtype))
    for name, factor in factors.items():
        out[name] = (out[name] * factor).astype(out[name].dtype)
    return out
```

```python
from contextlib import ExitStack

import concourse.bass as bass
from concourse import mybir

ALU = mybir.AluOpType
ACT = mybir.ActivationFunctionType
AX = mybir.AxisListType
F32 = mybir.dt.float32
F32R = mybir.dt.float32r
BF16 = mybir.dt.bfloat16

P = 128
B, S, E = 2, 512, 256
TOK = B * S
NH, NKV = 16, 4
D = E // NH
R = NH // NKV
F = 1024
KE = E // P
KF = F // P
C = S // P
T = TOK // P
NG = B * NKV
EPS = 1e-5
SCALE = float(D) ** -0.5
MASKED = -1.0e30

Q_PART = (0, 0, 0, 1, 1, 2)
K_PART = (0, 1, 2, 0, 1, 0)
TERMS = len(Q_PART)
MAX_ROW = TERMS * D
STACK = MAX_ROW + 2

TILES = [(b, what) for b in range(B) for what in ("kv", "q0", "q1", "f0", "f1")]
STACKED = [i for i, (b, what) in enumerate(TILES) if what[0] != "f"]
TRANSFORMED = [i for i, (b, what) in enumerate(TILES) if what[0] == "f"]

S_UNITS = [(3, (0, 1)), (3, (2, 3)), (0, (0, 1, 2, 3)), (1, (0, 1, 2, 3)), (2, (0, 1)), (2, (2, 3))]
NS = len(S_UNITS)
MT_UNIT = 2
NT = 5
FFN = [(b, n) for b in range(B) for n in range(KF)]
AHEAD = 2
GU_RING = 4


def psum_tile(i):
    return 4 + i % 4


def ffn_bank(u):
    return 6 - 2 * (u % 2)


def block_kernel(nc, x, xT, wqkv, wgu, wd, wo, vec, cst, yT, parts_dram):
    with ExitStack() as ctx:
        def sb(name, shape, dt, c=ctx):
            return c.enter_context(nc.sbuf_tensor(name, shape, dt))

        def sem(name):
            return ctx.enter_context(nc.semaphore(name))

        q_stack = sb("q_stack", [P, B * NH, S], BF16)
        k_stack = sb("k_stack", [P, NG, S], BF16)
        v_ones = sb("v_ones", [P, B, C, NKV, 32], F32)
        cst_sb = sb("cst_sb", [P, 3, P], F32)
        ident = cst_sb[:, 0, :]
        ident_bf = sb("ident_bf", [P, P], BF16)
        mask_bf = sb("mask_bf", [P, P], BF16)
        had = sb("had", [P, KE, E], F32R)
        vec_sb = sb("vec_sb", [P, 28], F32)
        su_ug = vec_sb[:, 0:2]
        s_gate_raw, s_up_raw = vec_sb[:, 2:10], vec_sb[:, 10:18]
        su_dp, s_dp_raw = vec_sb[:, 18:26], vec_sb[:, 26:28]
        s_gate = sb("s_gate", [P, KF], F32)
        s_up = sb("s_up", [P, KF], F32)
        s_dp = sb("s_dp", [P, KE], F32)
        half = sb("half", [P, C], F32)
        stats = sb("stats", [P, T, 6], F32)
        mv = sb("mv", [P, T, 2], F32)
        var_eps = sb("var_eps", [P, T], F32)
        rstd = sb("rstd", [P, T], F32)
        rowmax = sb("rowmax", [P, NG, C, R], F32)
        negmax = sb("negmax", [P, NG, C, 2, R], BF16)
        negmaxT = sb("negmaxT", [2 * R, 2, S], BF16)
        recip = sb("recip", [P, C, R], F32)
        wd_a = sb("wd_a", [P, KF, E], F32)
        wd_b = sb("wd_b", [P, KF, E], F32)
        h_sb = [sb("h_b0", [P, KF, S], F32), None]

        with ExitStack() as c:
            xh = sb("xh", [P, KE, TOK // 2], F32R, c)
            xl = sb("xl", [P, KE, TOK // 2], F32R, c)
            xh1 = sb("xh1", [P, KE, TOK // 2], F32R, c)
            xl1 = sb("xl1", [P, KE, TOK // 2], F32R, c)
        xh, xl = [xh, xh1], [xl, xl1]
        h_sb[1] = sb("h_b1", [P, KF, S], F32)

        with ExitStack() as c:
            x_sb = sb("x_sb", [P, T, E], F32, c)
        w2 = sb("w2", [P, KF, E], F32)

        with ExitStack() as c:
            part = sb("part", [P, len(STACKED), 3, S], BF16, c)
            rest = sb("rest", [P, 2, S], F32, c)
            vT = sb("vT", [P, B, S], F32, c)
            wqkv_sb = sb("wqkv_sb", [P, KE, 3 * P], F32, c)
            wqkv_h = sb("wqkv_h", [P, KE, 3 * P], F32R, c)
            wqkv_l = sb("wqkv_l", [P, KE, 3 * P], F32R, c)
            wgu_sb = sb("wgu_sb", [P, GU_RING, KE, 2 * P], F32, c)
            wgu_h = sb("wgu_h", [P, KE, 2 * F], F32R, c)
            wgu_l = sb("wgu_l", [P, KE, 2 * F], F32R, c)
            fh = sb("fh", [P, KE, TOK], F32R, c)
            fl = sb("fl", [P, KE, TOK], F32R, c)
            silu = sb("silu", [P, 2, S], F32, c)
        probs = sb("probs", [P, 2, NT, 2 * S], F32)
        acc = sb("acc", [P, KE, TOK], F32)
        o_sb = sb("o_sb", [P, T, E], F32)
        oT_sb = sb("oT_sb", [P, 2, S], F32)
        oh = sb("oh", [P, KE, TOK], F32R)
        ol = sb("ol", [P, KE, TOK], F32R)
        wo_sb = sb("wo_sb", [P, KE, E], F32)
        wo_h = sb("wo_h", [P, KE, E], F32R)
        wo_l = sb("wo_l", [P, KE, E], F32R)
        out_sb = sb("out_sb", [P, B * KE, S], F32)

        bank = ctx.enter_context(nc.psum_tensor("bank", [P, 8, S], F32))

        ld_x = [sem(f"ld_x{i}") for i in range(4)]
        ld_cst, ld_vec, ld_wqkv, ld_wd = sem("ld_cst"), sem("ld_vec"), sem("ld_wqkv"), sem("ld_wd")
        ld_wgu = [sem(f"ld_wgu{i}") for i in range(GU_RING)]
        ld_wo, ld_xT = sem("ld_wo"), sem("ld_xT")
        st_parts = [sem(f"st_parts{j}") for j in range(len(STACKED))]
        ld_stack = [sem(f"ld_stack{j}") for j in range(len(STACKED))]
        st_max = [sem(f"st_max{g}") for g in range(NG)]
        st_y = sem("st_y")
        consts_cast = sem("consts_cast")
        scales_ready = sem("scales_ready")
        had_ready = sem("had_ready")
        filled = sem("filled")
        stat_done = sem("stat_done")
        rstd_done = sem("rstd_done")
        norm_done = sem("norm_done")
        xT_done = sem("xT_done")
        xh_done, xl_done = sem("xh_done"), sem("xl_done")
        wqkv_hi, wqkv_lo = sem("wqkv_hi"), sem("wqkv_lo")
        wgu_hi, wgu_lo = sem("wgu_hi"), sem("wgu_lo")
        tile_done = sem("tile_done")
        tile_first = sem("tile_first")
        tile_rest = sem("tile_rest")
        part_m, part_l = sem("part_m"), sem("part_l")
        vT_done = sem("vT_done")
        v_turned = sem("v_turned")
        v_ready = sem("v_ready")
        s_done = sem("s_done")
        max_done = sem("max_done")
        negmax_done = sem("negmax_done")
        negmaxT_done = sem("negmaxT_done")
        gate_done, up_done = sem("gate_done"), sem("up_done")
        silu_done, h_done = sem("silu_done"), sem("h_done")
        stage_done = sem("stage_done")
        w2_made, w2_ready = sem("w2_made"), sem("w2_ready")
        t_done = sem("t_done")
        exp_done = sem("exp_done")
        probs_masked = sem("probs_masked")
        pv_done = sem("pv_done")
        oT_out = sem("oT_out")
        o_turned = sem("o_turned")
        recip_done, o_done = sem("recip_done"), sem("o_done")
        down_done = sem("down_done")
        acc_done = sem("acc_done")
        wo_hi, wo_lo = sem("wo_hi"), sem("wo_lo")
        ot_done = sem("ot_done")
        oh_done, ol_done = sem("oh_done"), sem("ol_done")
        attn_done = sem("attn_done")
        y_done = sem("y_done")

        block = ctx.enter_context(nc.Block())

        def toks(b):
            return slice(b * S, (b + 1) * S)

        @block.sync
        def _(sp):
            x_t = x.rearrange("(t p) e -> p t e", p=P)
            for i in range(4):
                sp.dma_start(x_sb[:, 2 * i:2 * i + 2, :], x_t[:, 2 * i:2 * i + 2, :]).then_inc(ld_x[i], 16)
            sp.dma_start(vec_sb[:, :], vec).then_inc(ld_vec, 16)
            sp.dma_start(wqkv_sb[:, :, :], wqkv.rearrange("(k p) n -> p k n", p=P)).then_inc(ld_wqkv, 16)
            wgu_t = wgu.rearrange("(k p) n -> p k n", p=P)

            def load_gate_up(n):
                if n >= GU_RING:
                    sp.wait_ge(wgu_hi, n - GU_RING + 1)
                    sp.wait_ge(wgu_lo, n - GU_RING + 1)
                sp.dma_start(wgu_sb[:, n % GU_RING, :, :],
                             wgu_t[:, :, n * 2 * P:(n + 1) * 2 * P]).then_inc(ld_wgu[n % GU_RING], 16)

            for n in range(GU_RING):
                load_gate_up(n)
            sp.dma_start(wd_a[:, :, :], wd.rearrange("(k p) n -> p k n", p=P)).then_inc(ld_wd, 16)

            def store_stack(j):
                b, what = TILES[STACKED[j]]
                sp.wait_ge(tile_first, STACKED[j] + 1)
                sp.wait_ge(part_m, j + 1)
                sp.wait_ge(part_l, j + 1)
                rows = slice(0, 64 if what == "kv" else P)
                sp.dma_start(parts_dram[j, rows], part[rows, j, :, :]).then_inc(st_parts[j], 16)

            def load_stack(j):
                b, what = TILES[STACKED[j]]
                sp.wait_ge(st_parts[j], 16)
                rows = slice(0, 64 if what == "kv" else P)
                src = parts_dram[j, rows].rearrange("(h d) a t -> a d h t", d=D)
                for blk in range(TERMS):
                    if what == "kv":
                        dst = k_stack[blk * D:(blk + 1) * D, b * NKV:(b + 1) * NKV, :]
                        a = K_PART[blk]
                    else:
                        h0 = b * NH + int(what[1]) * NH // 2
                        dst = q_stack[blk * D:(blk + 1) * D, h0:h0 + NH // 2, :]
                        a = Q_PART[blk]
                    sp.dma_start(dst, src[a]).then_inc(ld_stack[j], 16)

            for j in range(3):
                store_stack(j)
                if j:
                    load_stack(j - 1)
            load_stack(2)
            for n in range(GU_RING, KF):
                load_gate_up(n)
            for j in range(3, 6):
                store_stack(j)
                if j > 3:
                    load_stack(j - 1)
            load_stack(5)
            for g in range(NG):
                sp.wait_ge(negmaxT_done, g + 1)
                for p in range(2):
                    sp.dma_start(q_stack[MAX_ROW + p:MAX_ROW + p + 1, g * R:(g + 1) * R, :],
                                 negmaxT[p * R:(p + 1) * R, g % 2, :]).then_inc(st_max[g], 16)
            sp.wait_ge(h_done, len(FFN))
            sp.dma_start(acc[:, :, :], xT.rearrange("(k p) n -> p k n", p=P)).then_inc(ld_xT, 16)
            sp.dma_start(wo_sb[:, :, :], wo.rearrange("(k p) n -> p k n", p=P)).then_inc(ld_wo, 16)
            for i in range(B * KE):
                sp.wait_ge(y_done, i + 1)
                b, m = divmod(i, KE)
                sp.dma_start(yT[m * P:(m + 1) * P, toks(b)], out_sb[:, i, :]).then_inc(st_y, 16)
            sp.wait_ge(st_y, 16 * B * KE)

        @block.gpsimd
        def _(pool):
            pool.dma_start(cst_sb[:, :, :], cst.rearrange("(c p) n -> p c n", p=P)).then_inc(ld_cst, 16)
            pool.memset(half[:, :], -0.5).then_inc(filled, 1)
            pool.memset(v_ones[:, :, :, :, :], 1.0).then_inc(filled, 1)
            pool.wait_ge(filled, 2)
            pool.memset(k_stack[MAX_ROW:MAX_ROW + 2, :, :], 1.0).then_inc(filled, 1)
            pool.wait_ge(filled, 3)
            for b in range(B):
                pool.wait_ge(stat_done, 3 * (b + 1))
                pool.tensor_tensor(rstd[:, b * C:(b + 1) * C], var_eps[:, b * C:(b + 1) * C], half[:, :],
                                   ALU.pow).then_inc(rstd_done, 1)
                if b == 0:
                    pool.wait_ge(wqkv_hi, 1)
                    pool.wait_ge(ld_wqkv, 16)
                    pool.tensor_tensor(wqkv_l[:, :, :], wqkv_sb[:, :, :], wqkv_h[:, :, :].bitcast(F32),
                                       ALU.subtract).then_inc(wqkv_lo, 1)
            def gate_up_lo(n):
                pool.wait_ge(wgu_hi, n + 1)
                pool.wait_ge(ld_wgu[n % GU_RING], 16 * (n // GU_RING + 1))
                cols = slice(n * 2 * P, (n + 1) * 2 * P)
                pool.tensor_tensor(wgu_l[:, :, cols], wgu_sb[:, n % GU_RING, :, :],
                                   wgu_h[:, :, cols].bitcast(F32), ALU.subtract).then_inc(wgu_lo, 1)

            def hadamard_stage(s):
                src, dst = (wd_b, wd_a) if s % 2 else (wd_a, wd_b)
                if s:
                    pool.wait_ge(stage_done, 2 * s)
                else:
                    pool.wait_ge(ld_wd, 16)
                a = src[:, :, :].rearrange("p (u two w) n -> p two u (w n)", two=2, w=1 << s)
                o = dst[:, :, :].rearrange("p (u two w) n -> p two u (w n)", two=2, w=1 << s)
                pool.tensor_tensor(o[:, 0], a[:, 0], a[:, 1], ALU.add).then_inc(stage_done, 1)
                pool.tensor_tensor(o[:, 1], a[:, 0], a[:, 1], ALU.subtract).then_inc(stage_done, 1)

            for n in range(4):
                gate_up_lo(n)
            hadamard_stage(0)
            gate_up_lo(4)
            gate_up_lo(5)
            hadamard_stage(1)
            gate_up_lo(6)
            gate_up_lo(7)
            hadamard_stage(2)
            for i in range(NG * NT):
                g, k = divmod(i, NT)
                pool.wait_ge(exp_done, i + 1)
                u = probs[:, g % 2, k, :]
                if k < 2:
                    v, pattern = u.rearrange("p (h q) -> p h q", h=2)[:, :, 0:P], [[0, 2], [1, P]]
                elif k < 4:
                    v = u.rearrange("p (h q) -> p h q", h=2)[:, :, 0:2 * P]
                    pattern = [[0, 2], [0, 2], [1, P]]
                else:
                    v, pattern = u.rearrange("p (h q) -> p h q", h=4)[:, :, 0:P], [[0, 4], [1, P]]
                pool.affine_select(out=v, in_=v, pattern=pattern, compare_op=ALU.is_ge, fill=0.0, base=0,
                                   channel_multiplier=-1).then_inc(probs_masked, 1)

        @block.scalar
        def _(act):
            act.wait_ge(ld_wqkv, 16)
            act.copy(wqkv_h[:, :, :], wqkv_sb[:, :, :]).then_inc(wqkv_hi, 1)
            act.wait_ge(ld_cst, 16)
            act.copy(ident_bf[:, :], ident).then_inc(consts_cast, 1)
            act.copy(mask_bf[:, :], cst_sb[:, 2, :]).then_inc(consts_cast, 1)

            def gate_up_hi(n):
                act.wait_ge(ld_wgu[n % GU_RING], 16 * (n // GU_RING + 1))
                act.copy(wgu_h[:, :, n * 2 * P:(n + 1) * 2 * P],
                         wgu_sb[:, n % GU_RING, :, :]).then_inc(wgu_hi, 1)

            def x_hi(b, k):
                act.wait_ge(xT_done, KE * b + k + 1)
                act.copy(xh[b][:, k, :], bank[:, KE * b + k, :]).then_inc(xh_done, 1)

            def tile_hi(i):
                b, what = TILES[i]
                act.wait_ge(tile_done, i + 1)
                ps = bank[:, psum_tile(i), :]
                if what[0] == "f":
                    act.copy(fh[:, int(what[1]), toks(b)], ps).then_inc(tile_first, 1)
                    return
                j = STACKED.index(i)
                if what == "kv":
                    act.copy(vT[64:P, b, :], ps[64:P, :]).then_inc(vT_done, 1)
                    act.copy(part[0:64, j, 0, :], ps[0:64, :]).then_inc(tile_first, 1)
                else:
                    act.copy(part[:, j, 0, :], ps).then_inc(tile_first, 1)

            def mid_part(i):
                if TILES[i][1][0] == "f":
                    return
                j = STACKED.index(i)
                rows = slice(0, 64 if TILES[i][1] == "kv" else P)
                act.wait_ge(tile_rest, i + 1)
                act.copy(part[rows, j, 1, :], rest[rows, j % 2, :]).then_inc(part_m, 1)

            x_hi(0, 0)
            x_hi(0, 1)
            gate_up_hi(0)
            x_hi(1, 0)
            x_hi(1, 1)
            for i in range(len(TILES)):
                tile_hi(i)
                if i:
                    mid_part(i - 1)
                if i in (3, 4, 8):
                    gate_up_hi({3: 1, 4: 2, 8: 3}[i])
            mid_part(len(TILES) - 1)

            act.wait_ge(scales_ready, 3)
            for u, (b, n) in enumerate(FFN):
                if 4 + u < KF:
                    gate_up_hi(4 + u)
                act.wait_ge(gate_done, u + 1)
                if u >= 2:
                    act.wait_ge(h_done, u - 1)
                act.activation(silu[:, u % 2, :], bank[:, ffn_bank(u), :], ACT.Silu,
                               scale=s_gate[:, n:n + 1]).then_inc(silu_done, 1)

            def exps(i):
                g, k = divmod(i, NT)
                act.wait_ge(t_done, i + 1)
                if g >= 2:
                    act.wait_ge(pv_done, g - 1)
                act.activation(probs[:, g % 2, k, :], bank[:, 2 * (i % 2):2 * (i % 2) + 2, :], ACT.Exp,
                               scale=SCALE).then_inc(exp_done, 1)

            for i in range(NG * NT):
                exps(i)
                if i == 4:
                    act.wait_ge(ld_wo, 16)
                    act.copy(wo_h[:, :, :], wo_sb[:, :, :]).then_inc(wo_hi, 1)
            for i in range(B * KE):
                b, k = divmod(i, KE)
                act.wait_ge(ot_done, i + 1)
                act.copy(oh[:, k, toks(b)], bank[:, k, :]).then_inc(oh_done, 1)

        @block.vector
        def _(dve):
            def statistics(b):
                for t in range(b * C, (b + 1) * C):
                    dve.wait_ge(ld_x[t // 2], 16)
                    ins = dve.bn_stats(stats[:, t, :], x_sb[:, t, :])
                ins.then_inc(stat_done, 1)
                dve.wait_ge(stat_done, 3 * b + 1)
                for t in range(b * C, (b + 1) * C):
                    ins = dve.bn_aggr(mv[:, t, :], stats[:, t, :])
                ins.then_inc(stat_done, 1)
                dve.wait_ge(stat_done, 3 * b + 2)
                dve.tensor_scalar(var_eps[:, b * C:(b + 1) * C], mv[:, b * C:(b + 1) * C, 1], EPS, None,
                                  ALU.add).then_inc(stat_done, 1)

            def normalise(b):
                dve.wait_ge(rstd_done, b + 1)
                for t in range(b * C, (b + 1) * C):
                    dve.tensor_scalar(x_sb[:, t, :], x_sb[:, t, :], mv[:, t, 0:1], rstd[:, t:t + 1],
                                      ALU.subtract, ALU.mult).then_inc(norm_done, 1)

            def x_lo(b, k):
                dve.wait_ge(xh_done, KE * b + k + 1)
                dve.tensor_tensor(xl[b][:, k, :], bank[:, KE * b + k, :], xh[b][:, k, :].bitcast(F32),
                                  ALU.subtract).then_inc(xl_done, 1)

            def tile_lo(i):
                b, what = TILES[i]
                dve.wait_ge(tile_first, i + 1)
                ps = bank[:, psum_tile(i), :]
                if what[0] == "f":
                    m = int(what[1])
                    dve.tensor_tensor(fl[:, m, toks(b)], ps, fh[:, m, toks(b)].bitcast(F32),
                                      ALU.subtract).then_inc(tile_rest, 1)
                    return
                j = STACKED.index(i)
                rows = slice(0, 64 if what == "kv" else P)
                if j >= 2:
                    dve.wait_ge(part_l, j - 1)
                dve.tensor_tensor(rest[rows, j % 2, :], ps[rows, :], part[rows, j, 0, :],
                                  ALU.subtract).then_inc(tile_rest, 1)

            def low_part(i):
                if TILES[i][1][0] == "f":
                    return
                j = STACKED.index(i)
                rows = slice(0, 64 if TILES[i][1] == "kv" else P)
                dve.wait_ge(part_m, j + 1)
                dve.tensor_tensor(part[rows, j, 2, :], rest[rows, j % 2, :], part[rows, j, 1, :],
                                  ALU.subtract).then_inc(part_l, 1)

            def v_out(b):
                dve.wait_ge(v_turned, b + 1)
                dve.wait_ge(filled, 2)
                dve.tensor_copy(v_ones[:, b, :, :, 0:D],
                                bank[:, 2 * b, 0:E].rearrange("p (c g d) -> p c g d", c=C, g=NKV)
                                ).then_inc(v_ready, 1)

            statistics(0)
            dve.wait_ge(ld_cst, 16)
            dve.wait_ge(ld_vec, 16)
            for k in range(KE):
                for m in range(KE):
                    dve.tensor_scalar(had[:, k, m * P:(m + 1) * P], cst_sb[:, 1, :], su_ug[:, k:k + 1],
                                      -1.0 if k and m else 1.0, ALU.mult, ALU.mult).then_inc(had_ready, 1)
            normalise(0)
            statistics(1)
            x_lo(0, 0)
            x_lo(0, 1)
            normalise(1)
            dve.tensor_scalar(s_gate[:, :], s_gate_raw, 1.0 / 16, None, ALU.mult).then_inc(scales_ready, 1)
            dve.scalar_tensor_tensor(s_up[:, :], s_up_raw, 1.0 / 16, su_dp, ALU.mult,
                                     ALU.mult).then_inc(scales_ready, 1)
            dve.tensor_scalar(s_dp[:, :], s_dp_raw, 1.0 / 32, None, ALU.mult).then_inc(scales_ready, 1)
            x_lo(1, 0)
            x_lo(1, 1)
            for i in range(len(TILES)):
                tile_lo(i)
                if i:
                    low_part(i - 1)
                if i == 3:
                    v_out(0)
                if i == 8:
                    v_out(1)
            dve.wait_ge(scales_ready, 3)

            def unit_max(g, k):
                i = g * NS + k
                c, heads = S_UNITS[k]
                dve.wait_ge(s_done, i + 1)
                u = bank[:, 2 * (i % 2):2 * (i % 2) + 2, :]
                n = P * (c + 1)
                flat = u.rearrange("p u n -> p (u n)")
                if c < 2:
                    v = flat[:, 0:R * n].rearrange("p (h n) -> p h n", n=n)
                else:
                    v = u[:, :, 0:n]
                ins = dve.tensor_reduce(rowmax[:, g, c, heads[0]:heads[-1] + 1], v, AX.X, ALU.max)
                if k == MT_UNIT and g:
                    turned_max(g - 1, u[:, 1, :])
                    return
                ins.then_inc(max_done, 1)

            def turned_max(g, ps):
                if g >= 2:
                    dve.wait_ge(st_max[g - 2], 32)
                dve.tensor_copy(negmaxT[:, g % 2, :], ps.bitcast(BF16)[0:2 * R, 0:S]
                                ).then_inc(negmaxT_done, 1)
                dve.wait_ge(negmaxT_done, g + 1)
                dve.sem_inc(max_done, 1)

            def negated_max(g):
                dve.wait_ge(max_done, NS * (g + 1))
                dve.tensor_scalar(negmax[:, g, :, 0, :], rowmax[:, g, :, :], -1.0, None,
                                  ALU.mult).then_inc(negmax_done, 1)
                dve.wait_ge(negmax_done, 2 * g + 1)
                dve.scalar_tensor_tensor(negmax[:, g, :, 1, :], rowmax[:, g, :, :], -1.0,
                                         negmax[:, g, :, 0, :], ALU.mult, ALU.subtract
                                         ).then_inc(negmax_done, 1)

            def gated(u):
                b, n = FFN[u]
                dve.wait_ge(up_done, u + 1)
                dve.wait_ge(silu_done, u + 1)
                dve.scalar_tensor_tensor(h_sb[b][:, n, :], bank[:, ffn_bank(u) + 1, :], s_up[:, n:n + 1],
                                         silu[:, u % 2, :], ALU.mult, ALU.mult).then_inc(h_done, 1)

            for u in range(AHEAD):
                gated(u)
            for g in range(NG):
                for k in range(NS):
                    unit_max(g, k)
                    if k == 2 and 2 * g + AHEAD < len(FFN):
                        gated(2 * g + AHEAD)
                negated_max(g)
                if 2 * g + AHEAD + 1 < len(FFN):
                    gated(2 * g + AHEAD + 1)
            dve.wait_ge(s_done, NG * NS + 1)
            turned_max(NG - 1, bank[:, 1, :])

            for q in range(4):
                dve.wait_ge(w2_made, q + 1)
                dve.tensor_copy(w2[:, 2 * q:2 * q + 2, :],
                                bank[:, 4 + q, :].rearrange("p (k n) -> p k n", k=2)).then_inc(w2_ready, 1)

            def oT(g):
                dve.wait_ge(pv_done, g + 1)
                dve.tensor_copy(oT_sb[:, g % 2, :], bank[:, 4 + g % 2, :]).then_inc(oT_out, 1)

            def normalised(g):
                b, kv = divmod(g, NKV)
                dve.wait_ge(o_turned, g + 1)
                v = bank[:, 6, :].rearrange("p (c r w) -> p c r w", c=C, r=R)
                dve.reciprocal(recip[:, :, :], v[:, :, :, D]).then_inc(recip_done, 1)
                dve.wait_ge(recip_done, g + 1)
                o = o_sb[:, b * C:(b + 1) * C, kv * R * D:(kv + 1) * R * D]
                dve.tensor_tensor(o.rearrange("p c (r d) -> p c r d", r=R), v[:, :, :, 0:D],
                                  recip[:, :, :].unsqueeze(3).to_broadcast([P, C, R, D]),
                                  ALU.mult).then_inc(o_done, 1)

            def add_ffn(d):
                b, m = divmod(d, KE)
                dve.wait_ge(down_done, d + 1)
                dve.wait_ge(ld_xT, 16)
                dve.scalar_tensor_tensor(acc[:, m, toks(b)], bank[:, 7, :], s_dp[:, m:m + 1],
                                         acc[:, m, toks(b)], ALU.mult, ALU.add).then_inc(acc_done, 1)

            dve.wait_ge(wo_hi, 1)
            dve.tensor_tensor(wo_l[:, :, :], wo_sb[:, :, :], wo_h[:, :, :].bitcast(F32),
                              ALU.subtract).then_inc(wo_lo, 1)
            for p in range(1, NG):
                if p >= 2:
                    normalised(p - 2)
                if p in (2, 5):
                    add_ffn(p // 3)
                oT(p - 1)
            add_ffn(2)
            normalised(NG - 2)
            oT(NG - 1)
            normalised(NG - 1)
            add_ffn(3)
            for b in range(B):
                for k in range(KE):
                    dve.wait_ge(oh_done, KE * b + k + 1)
                    dve.tensor_tensor(ol[:, k, toks(b)], bank[:, k, :], oh[:, k, toks(b)].bitcast(F32),
                                      ALU.subtract).then_inc(ol_done, 1)
            for i in range(B * KE):
                b, m = divmod(i, KE)
                dve.wait_ge(attn_done, i + 1)
                dve.wait_ge(acc_done, i + 1)
                dve.tensor_tensor(out_sb[:, i, :], bank[:, 2 + i % 2, :], acc[:, m, toks(b)],
                                  ALU.add).then_inc(y_done, 1)

        @block.tensor
        def _(pe):
            def three_passes(out, wh, wl, vh, vl):
                n = len(wh)
                for k in range(n):
                    pe.matmul(out, wh[k], vh[k], start=k == 0, stop=False)
                    pe.matmul(out, wh[k], vl[k], start=False, stop=False)
                    ins = pe.matmul(out, wl[k], vh[k], start=False, stop=k == n - 1)
                return ins

            def turn_x(b):
                for k in range(KE):
                    for c in range(C):
                        t = b * C + c
                        if k == 0:
                            pe.wait_ge(norm_done, t + 1)
                        ins = pe.transpose(bank[:, KE * b + k, c * P:(c + 1) * P],
                                           x_sb[:, t, k * P:(k + 1) * P], ident)
                    ins.then_inc(xT_done, 1)

            def projection(i):
                b, what = TILES[i]
                if i >= 4:
                    pe.wait_ge(tile_first, i - 3)
                    pe.wait_ge(tile_rest, i - 3)
                    if TILES[i - 4][1] == "kv":
                        pe.wait_ge(vT_done, TILES[i - 4][0] + 1)
                ks = range(KE)
                if what[0] == "f":
                    m = slice(int(what[1]) * P, (int(what[1]) + 1) * P)
                    out = bank[:, psum_tile(i), :]
                    for k in ks:
                        pe.matmul(out, had[:, k, m], xh[b][:, k, :], start=k == 0, stop=False)
                        ins = pe.matmul(out, had[:, k, m], xl[b][:, k, :], start=False, stop=k == KE - 1)
                else:
                    m = {"q0": 0, "q1": 1, "kv": 2}[what]
                    m = slice(m * P, (m + 1) * P)
                    ins = three_passes(bank[:, psum_tile(i), :], [wqkv_h[:, k, m] for k in ks],
                                       [wqkv_l[:, k, m] for k in ks], [xh[b][:, k, :] for k in ks],
                                       [xl[b][:, k, :] for k in ks])
                ins.then_inc(tile_done, 1)

            def turn_v(b):
                pe.wait_ge(vT_done, b + 1)
                for c in range(C):
                    ins = pe.transpose(bank[:, 2 * b, c * 64:(c + 1) * 64],
                                       vT[64:P, b, c * P:(c + 1) * P], ident[64:P, 64:P])
                ins.then_inc(v_turned, 1)

            pe.wait_ge(ld_cst, 16)
            turn_x(0)
            pe.wait_ge(wqkv_lo, 1)
            pe.wait_ge(xl_done, KE)
            for i in range(0, 3):
                projection(i)
            turn_x(1)
            turn_v(0)
            pe.wait_ge(had_ready, KE * KE)
            for i in range(3, 5):
                projection(i)
            pe.wait_ge(xl_done, 2 * KE)
            for i in range(5, 10):
                projection(i)
                if i == 6:
                    turn_v(1)

            def gate_or_up(u, which):
                b, n = FFN[u]
                if which == 0:
                    pe.wait_ge(wgu_lo, n + 1)
                    if u >= 2:
                        pe.wait_ge(silu_done, u - 1)
                elif u >= 2:
                    pe.wait_ge(h_done, u - 1)
                if u < 2:
                    pe.wait_ge(tile_rest, 7 + 2 * u + which)
                m = slice((2 * n + which) * P, (2 * n + which + 1) * P)
                ks = range(KE)
                ins = three_passes(bank[:, ffn_bank(u) + which, :], [wgu_h[:, k, m] for k in ks],
                                   [wgu_l[:, k, m] for k in ks], [fh[:, k, toks(b)] for k in ks],
                                   [fl[:, k, toks(b)] for k in ks])
                ins.then_inc(up_done if which else gate_done, 1)

            def turn_max(g, out):
                pe.wait_ge(negmax_done, 2 * (g + 1))
                for c in range(C):
                    ins = pe.transpose(out.bitcast(BF16)[0:2 * R, c * P:(c + 1) * P],
                                       negmax[:, g, c, :, :].rearrange("p a r -> p (a r)"), ident_bf[:, :])
                return ins

            def scores(g, k):
                b, kv = divmod(g, NKV)
                i = g * NS + k
                c, heads = S_UNITS[k]
                n = P * (c + 1)
                if i >= 2:
                    pe.wait_ge(max_done, i - 1)
                if k == 0:
                    pe.wait_ge(ld_stack[3 * b], 16 * TERMS)
                    pe.wait_ge(ld_stack[3 * b + 1 + kv // 2], 16 * TERMS)
                if k == MT_UNIT and g:
                    turn_max(g - 1, bank[:, 2 * (i % 2) + 1, :])
                u = bank[:, 2 * (i % 2):2 * (i % 2) + 2, :].rearrange("p u n -> p (u n)")
                for a, r in enumerate(heads):
                    at = a * (n if c < 2 else S)
                    pe.matmul(u[:, at:at + n], q_stack[0:MAX_ROW, g * R + r, c * P:(c + 1) * P],
                              k_stack[0:MAX_ROW, g, 0:n], start=True, stop=False)
                    ins = pe.matmul(u[:, at + n - P:at + n], ident_bf[:, :], mask_bf[:, :],
                                    start=False, stop=True)
                ins.then_inc(s_done, 1)

            pe.wait_ge(consts_cast, 2)
            for u in range(AHEAD):
                gate_or_up(u, 0)
                gate_or_up(u, 1)
            pe.wait_ge(v_ready, 2)
            for g in range(NG):
                for k in range(NS):
                    scores(g, k)
                    u = 2 * g + AHEAD + k // 3
                    if u < len(FFN) and k in (1, 2, 3, 5):
                        gate_or_up(u, k in (2, 5))
            pe.wait_ge(max_done, NG * NS)
            turn_max(NG - 1, bank[:, 1, :]).then_inc(s_done, 1)

            pe.wait_ge(stage_done, 6)
            pe.wait_ge(h_done, len(FFN))
            for q in range(4):
                for j in (2 * q, 2 * q + 1):
                    ins = pe.matmul(bank[:, 4 + q, (j % 2) * E:(j % 2 + 1) * E], cst_sb[:, 1, :],
                                    wd_b[:, j, :], start=True, stop=True)
                ins.then_inc(w2_made, 1)

            def transposed_scores(g, k):
                i = g * NT + k
                if i >= 2:
                    pe.wait_ge(exp_done, i - 1)
                if k == 0:
                    pe.wait_ge(st_max[g], 32)
                u = bank[:, 2 * (i % 2):2 * (i % 2) + 2, :].rearrange("p u n -> p (u n)")
                if k < 2:
                    blocks = [(2 * k + a, 0, a * S) for a in range(2)]
                elif k < 4:
                    blocks = [(2 * (k - 2) + a, j, a * S + at) for a in range(2) for j, at in ((3, 0), (1, P))]
                else:
                    blocks = [(a, 2, a * 2 * P) for a in range(R)]
                for r, j, at in blocks:
                    ins = pe.matmul(u[:, at:at + S - j * P], k_stack[0:STACK, g, j * P:(j + 1) * P],
                                    q_stack[0:STACK, g * R + r, j * P:S], start=True, stop=True)
                ins.then_inc(t_done, 1)

            def weighted_values(g, j):
                b, kv = divmod(g, NKV)
                pe.wait_ge(probs_masked, g * NT + {0: 2, 1: 4, 3: 4, 2: 5}[j])
                if j == 0 and g >= 2:
                    pe.wait_ge(oT_out, g - 1)
                for r in range(R):
                    unit, at = {0: (r // 2, r % 2 * S), 1: (2 + r // 2, r % 2 * S + P),
                                3: (2 + r // 2, r % 2 * S), 2: (4, r * 2 * P)}[j]
                    ins = pe.matmul(bank[32 * r:32 * (r + 1), 4 + g % 2, j * P:S], v_ones[:, b, j, kv, :],
                                    probs[:, g % 2, unit, at:at + S - j * P], start=j == 0, stop=j == 2,
                                    skip_group_check=True)
                if j == 2:
                    ins.then_inc(pv_done, 1)

            def turn_o(g):
                pe.wait_ge(oT_out, g + 1)
                if g:
                    pe.wait_ge(o_done, g)
                for c in range(C):
                    ins = pe.transpose(bank[:, 6, c * P:(c + 1) * P], oT_sb[:, g % 2, c * P:(c + 1) * P], ident)
                ins.then_inc(o_turned, 1)

            def down():
                for d in range(B * KE):
                    b, m = divmod(d, KE)
                    for n in range(KF):
                        if n == 0 and d:
                            pe.wait_ge(acc_done, d)
                        ins = pe.matmul(bank[:, 7, :], w2[:, n, m * P:(m + 1) * P], h_sb[b][:, n, :],
                                        start=n == 0, stop=n == KF - 1)
                        if n == KF - 1:
                            ins.then_inc(down_done, 1)
                        yield

            steps = down()
            pe.wait_ge(w2_ready, 4)
            PV_ORDER = (0, 1, 3, 2)
            for g in range(NG):
                for k in range(NT):
                    transposed_scores(g, k)
                    if g and k < 4:
                        weighted_values(g - 1, PV_ORDER[k])
                    if g >= 2 and k == 1:
                        turn_o(g - 2)
                    if k in (0, 2, 4):
                        next(steps)
            turn_o(NG - 2)
            next(steps)
            for j in PV_ORDER:
                weighted_values(NG - 1, j)
            turn_o(NG - 1)
            for _ in steps:
                pass

            pe.wait_ge(exp_done, NG * NT)
            pe.wait_ge(wo_lo, 1)
            for b in range(B):
                pe.wait_ge(o_done, NKV * (b + 1))
                if b:
                    pe.wait_ge(ol_done, KE)
                for k in range(KE):
                    for c in range(C):
                        ins = pe.transpose(bank[:, k, c * P:(c + 1) * P],
                                           o_sb[:, b * C + c, k * P:(k + 1) * P], ident)
                    ins.then_inc(ot_done, 1)
            for b in range(B):
                pe.wait_ge(ol_done, KE * (b + 1))
                for m in range(KE):
                    if b:
                        pe.wait_ge(y_done, m + 1)
                    ks = range(KE)
                    ms = slice(m * P, (m + 1) * P)
                    three_passes(bank[:, 2 + m, :], [wo_h[:, k, ms] for k in ks], [wo_l[:, k, ms] for k in ks],
                                 [oh[:, k, toks(b)] for k in ks],
                                 [ol[:, k, toks(b)] for k in ks]).then_inc(attn_done, 1)


def kernel(L0_attn_x, L0_attn_Wq, L0_attn_Wk, L0_attn_Wv, L0_attn_Wo, L0_ffn_SU_ug, L0_ffn_SU_dp,
           L0_ffn_Wscale_ug, L0_ffn_Wscale_dp, L0_ffn_W_up, L0_ffn_W_gate, L0_ffn_W_down):
    import numpy as np
    import concourse.bacc as bacc
    from concourse.bass_utils import run_bass_kernel_spmd

    def tiles(v):
        return np.asarray(v).reshape(-1, P).T

    x = np.ascontiguousarray(L0_attn_x).reshape(TOK, E)
    gate_up = np.stack([np.asarray(L0_ffn_W_gate).reshape(KF, P, E), np.asarray(L0_ffn_W_up).reshape(KF, P, E)], 1)
    wscale = np.asarray(L0_ffn_Wscale_ug)
    i = np.arange(P)
    hadamard = np.array([[1.0]], np.float32)
    while hadamard.shape[0] < P:
        hadamard = np.block([[hadamard, hadamard], [hadamard, -hadamard]])
    constants = np.concatenate([np.eye(P), hadamard, np.where(i[None, :] > i[:, None], MASKED, 0.0)], 0)
    arrays = {
        "x": x,
        "xT": x.T,
        "wqkv": np.concatenate([np.asarray(a) for a in (L0_attn_Wq, L0_attn_Wk, L0_attn_Wv)], 1),
        "wgu": gate_up.reshape(2 * F, E).T,
        "wd": np.asarray(L0_ffn_W_down).T,
        "wo": np.asarray(L0_attn_Wo),
        "vec": np.concatenate([tiles(L0_ffn_SU_ug), tiles(wscale[F:]), tiles(wscale[:F]), tiles(L0_ffn_SU_dp),
                               tiles(L0_ffn_Wscale_dp)], 1),
        "cst": constants.astype(np.float32),
    }
    arrays = {name: np.ascontiguousarray(a) for name, a in arrays.items()}
    nc = bacc.Bacc("TRN2", target_bir_lowering=False, num_devices=1)
    ins = [nc.dram_tensor(f"in_{name}", a.shape, mybir.dt.from_np(a.dtype), kind="ExternalInput").ap()
           for name, a in arrays.items()]
    out = nc.dram_tensor("out_yT", (E, TOK), F32, kind="ExternalOutput").ap()
    parts = nc.dram_tensor("parts", (6, P, 3, S), BF16, kind="Internal").ap()
    block_kernel(nc, *ins, out, parts)
    r = run_bass_kernel_spmd(nc, [{f"in_{name}": a for name, a in arrays.items()}], core_ids=[0])
    return np.ascontiguousarray(r.results[0]["out_yT"].T).reshape(B, S, E)
```

```python
from contextlib import ExitStack

import concourse.bass as bass
from concourse import mybir

ALU = mybir.AluOpType
ACT = mybir.ActivationFunctionType
AX = mybir.AxisListType
F32 = mybir.dt.float32
F32R = mybir.dt.float32r
BF16 = mybir.dt.bfloat16

P = 128
B, S, E = 2, 512, 256
TOK = B * S
NH, NKV = 16, 4
D = E // NH
R = NH // NKV
F = 1024
KE = E // P
KF = F // P
C = S // P
T = TOK // P
NG = B * NKV
EPS = 1e-5
SCALE = float(D) ** -0.5
MASKED = -1.0e30

Q_PART = (0, 0, 0, 1, 1, 2)
K_PART = (0, 1, 2, 0, 1, 0)
TERMS = len(Q_PART)
MAX_ROW = TERMS * D
STACK = MAX_ROW + 2
PV_ORDER = (0, 1, 3, 2)

TILES = [(b, what) for b in range(B) for what in ("kv", "q0", "q1", "f0", "f1")]
TILE_BANK = (4, 5, 6, 7, 1, 0, 2, 3, 1, 0)
STACKED = [i for i, (b, what) in enumerate(TILES) if what[0] != "f"]
TURN_BANK = ((0, 1), (2, 3))
V_BANK = (0, 2)
HAD_BANK = (2, 3, 6, 7)

OPENING = [("T", 0), ("H", 0), (0,), (1,), ("V", 0), ("T", 1), (2,), (3,), (4,), (5,), (6,), ("F", 0),
           ("F", 1), (7,), (8,), ("F", 2), (9,), ("V", 1), ("F", 3)]
AHEAD = sum(step[0] == "F" for step in OPENING)

S_UNITS = [(3, (0, 1)), (3, (2, 3)), (0, (0, 1, 2, 3)), (1, (0, 1, 2, 3)), (2, (0, 1)), (2, (2, 3))]
NS = len(S_UNITS)
MT_UNIT = 2
NT = 5
FFN = [(b, n) for b in range(B) for n in range(KF)]
EARLY = 2
H_RING = 3
SLOTS = (NG - EARLY) * NT
PAUSE = 3 * KF
GU_RING = 4


def ffn_bank(u):
    return 4 + 2 * (u % 2)


def t_bank(i):
    return 4 + 2 * (i % 2)


def split_after(slot):
    n, r = divmod(slot + 4, 3)
    return n if r == 0 and n >= 0 else None


LAST_SPLIT = max(split_after(slot) or 0 for slot in range(SLOTS))
POOL_SPLITS = 2


def block_kernel(nc, x, xT, wqkv, wgu, wd, wo, vec, cst, yT, parts_dram):
    with ExitStack() as ctx:
        def sb(name, shape, dt, c=ctx):
            return c.enter_context(nc.sbuf_tensor(name, shape, dt))

        def sem(name):
            return ctx.enter_context(nc.semaphore(name))

        q_stack = sb("q_stack", [P, B * NH, S], BF16)
        k_stack = sb("k_stack", [P, NG, S], BF16)
        v_ones = sb("v_ones", [P, B, C, NKV, 32], F32)
        cst_sb = sb("cst_sb", [P, 3, P], F32)
        ident = cst_sb[:, 0, :]
        ident_bf = sb("ident_bf", [P, P], BF16)
        mask_bf = sb("mask_bf", [P, P], BF16)
        had = sb("had", [P, KE, E], F32R)
        vec_sb = sb("vec_sb", [P, 28], F32)
        su_ug = vec_sb[:, 0:2]
        s_gate_raw, s_up_raw = vec_sb[:, 2:10], vec_sb[:, 10:18]
        su_dp, s_dp_raw = vec_sb[:, 18:26], vec_sb[:, 26:28]
        s_gate = sb("s_gate", [P, KF], F32)
        s_up = sb("s_up", [P, KF], F32)
        s_dp = sb("s_dp", [P, KE], F32)
        half = sb("half", [P, 2], F32)
        table_warm = sb("table_warm", [P, 1], F32)
        stats = sb("stats", [P, T, 6], F32)
        mv = sb("mv", [P, T, 2], F32)
        var_eps = sb("var_eps", [P, T], F32)
        rstd = sb("rstd", [P, T], F32)
        rowmax = sb("rowmax", [P, NG, C, R], F32)
        negmax = sb("negmax", [P, NG, C, 2, R], BF16)
        negmaxT = sb("negmaxT", [2 * R, 2, S], BF16)
        recip = sb("recip", [P, C, R], F32)
        wd_b = sb("wd_b", [P, KF, E], F32)
        h_sb = [sb("h_b0", [P, KF, S], F32), None]

        with ExitStack() as c:
            xh = sb("xh", [P, KE, TOK // 2], F32R, c)
            xl = sb("xl", [P, KE, TOK // 2], F32R, c)
            xh1 = sb("xh1", [P, KE, TOK // 2], F32R, c)
            xl1 = sb("xl1", [P, KE, TOK // 2], F32R, c)
        xh, xl = [xh, xh1], [xl, xl1]
        h_sb[1] = sb("h_b1", [P, KF, S], F32)

        with ExitStack() as c:
            wd_a = sb("wd_a", [P, KF, E], F32, c)
        w2_h = sb("w2_h", [P, KF, E], F32R)

        with ExitStack() as c:
            x_sb = sb("x_sb", [P, T, E], F32, c)
        w2_l = sb("w2_l", [P, KF, E], F32R)

        with ExitStack() as c:
            part = sb("part", [P, len(STACKED), 3, S], BF16, c)
            rest = sb("rest", [P, 2, S], F32, c)
            vT = sb("vT", [P, B, S], F32, c)
            wqkv_sb = sb("wqkv_sb", [P, KE, 3 * P], F32, c)
            wqkv_h = sb("wqkv_h", [P, KE, 3 * P], F32R, c)
            wqkv_l = sb("wqkv_l", [P, KE, 3 * P], F32R, c)
            wgu_sb = sb("wgu_sb", [P, GU_RING, KE, 2 * P], F32, c)
            wgu_h = sb("wgu_h", [P, KE, 2 * F], F32R, c)
            wgu_l = sb("wgu_l", [P, KE, 2 * F], F32R, c)
            fh = sb("fh", [P, KE, TOK], F32R, c)
            fl = sb("fl", [P, KE, TOK], F32R, c)
            silu = sb("silu", [P, 2, S], F32, c)
            up = sb("up", [P, 2, S], F32, c)
        probs = sb("probs", [P, 2, NT, 2 * S], F32)
        acc = sb("acc", [P, KE, TOK], F32)
        o_sb = sb("o_sb", [P, T, E], F32)
        with ExitStack() as c:
            oT_sb = sb("oT_sb", [P, 2, S], F32, c)
        out_sb = sb("out_sb", [P, 2, S], F32)
        h_hi = sb("h_hi", [P, H_RING, S], F32R)
        h_lo = sb("h_lo", [P, H_RING, S], F32R)
        oh = sb("oh", [P, KE, TOK], F32R)
        ol = sb("ol", [P, KE, TOK], F32R)
        wo_sb = sb("wo_sb", [P, KE, E], F32)
        wo_h = sb("wo_h", [P, KE, E], F32R)
        wo_l = sb("wo_l", [P, KE, E], F32R)

        bank = ctx.enter_context(nc.psum_tensor("bank", [P, 8, S], F32))

        ld_x = [sem(f"ld_x{i}") for i in range(4)]
        ld_cst, ld_vec, ld_wqkv, ld_wd = sem("ld_cst"), sem("ld_vec"), sem("ld_wqkv"), sem("ld_wd")
        ld_wgu = [sem(f"ld_wgu{i}") for i in range(GU_RING)]
        ld_wo, ld_xT = sem("ld_wo"), sem("ld_xT")
        st_parts = [sem(f"st_parts{j}") for j in range(len(STACKED))]
        ld_stack = [sem(f"ld_stack{j}") for j in range(len(STACKED))]
        st_max = [sem(f"st_max{g}") for g in range(NG)]
        st_y = [sem(f"st_y{i}") for i in range(B * KE)]
        consts_cast = sem("consts_cast")
        scales_ready = sem("scales_ready")
        had_ready = sem("had_ready")
        filled = sem("filled")
        stat_done = sem("stat_done")
        rstd_done = sem("rstd_done")
        norm_done = sem("norm_done")
        xT_done = sem("xT_done")
        xh_done, xl_done = sem("xh_done"), sem("xl_done")
        wqkv_hi, wqkv_lo = sem("wqkv_hi"), sem("wqkv_lo")
        wgu_hi, wgu_lo = sem("wgu_hi"), sem("wgu_lo")
        tile_done = sem("tile_done")
        tile_first = sem("tile_first")
        tile_rest = sem("tile_rest")
        part_m, part_l = sem("part_m"), sem("part_l")
        vT_done = sem("vT_done")
        v_turned = sem("v_turned")
        v_ready = sem("v_ready")
        s_done = sem("s_done")
        max_done = sem("max_done")
        negmax_done = sem("negmax_done")
        negmaxT_done = sem("negmaxT_done")
        gate_done, up_done = sem("gate_done"), sem("up_done")
        silu_done, h_done = sem("silu_done"), sem("h_done")
        up_out = sem("up_out")
        stage_done = sem("stage_done")
        had_made, had_out = sem("had_made"), sem("had_out")
        w2_hi, w2_lo = sem("w2_hi"), sem("w2_lo")
        h_hi_done, h_lo_done = sem("h_hi_done"), sem("h_lo_done")
        h_used = sem("h_used")
        t_done = sem("t_done")
        exp_done = sem("exp_done")
        probs_masked = sem("probs_masked")
        pv_done = sem("pv_done")
        oT_out = sem("oT_out")
        o_turned = sem("o_turned")
        recip_done, o_done = sem("recip_done"), sem("o_done")
        acc_done = sem("acc_done")
        wo_hi, wo_lo = sem("wo_hi"), sem("wo_lo")
        ot_done = sem("ot_done")
        oh_done, ol_done = sem("oh_done"), sem("ol_done")
        attn_done = sem("attn_done")
        y_done = sem("y_done")

        block = ctx.enter_context(nc.Block())

        def toks(b):
            return slice(b * S, (b + 1) * S)

        @block.sync
        def _(sp):
            x_t = x.rearrange("(t p) e -> p t e", p=P)
            for i in range(2):
                sp.dma_start(x_sb[:, 2 * i:2 * i + 2, :], x_t[:, 2 * i:2 * i + 2, :]).then_inc(ld_x[i], 16)
            sp.dma_start(wd_b[:, :, :], wd.rearrange("(k p) n -> p k n", p=P)).then_inc(ld_wd, 16)
            sp.dma_start(wqkv_sb[:, :, :], wqkv.rearrange("(k p) n -> p k n", p=P)).then_inc(ld_wqkv, 16)
            for i in range(2, 4):
                sp.dma_start(x_sb[:, 2 * i:2 * i + 2, :], x_t[:, 2 * i:2 * i + 2, :]).then_inc(ld_x[i], 16)
            wgu_t = wgu.rearrange("(k p) n -> p k n", p=P)

            def load_gate_up(n):
                if n >= GU_RING:
                    sp.wait_ge(wgu_hi, n - GU_RING + 1)
                    sp.wait_ge(wgu_lo, n - GU_RING + 1)
                sp.dma_start(wgu_sb[:, n % GU_RING, :, :],
                             wgu_t[:, :, n * 2 * P:(n + 1) * 2 * P]).then_inc(ld_wgu[n % GU_RING], 16)

            for n in range(GU_RING):
                load_gate_up(n)
            def store_stack(j):
                b, what = TILES[STACKED[j]]
                sp.wait_ge(tile_first, STACKED[j] + 1)
                sp.wait_ge(part_m, j + 1)
                sp.wait_ge(part_l, j + 1)
                rows = slice(0, 64 if what == "kv" else P)
                sp.dma_start(parts_dram[j, rows], part[rows, j, :, :]).then_inc(st_parts[j], 16)

            def load_stack(j):
                b, what = TILES[STACKED[j]]
                sp.wait_ge(st_parts[j], 16)
                rows = slice(0, 64 if what == "kv" else P)
                src = parts_dram[j, rows].rearrange("(h d) a t -> a d h t", d=D)
                for blk in range(TERMS):
                    if what == "kv":
                        dst = k_stack[blk * D:(blk + 1) * D, b * NKV:(b + 1) * NKV, :]
                        a = K_PART[blk]
                    else:
                        h0 = b * NH + int(what[1]) * NH // 2
                        dst = q_stack[blk * D:(blk + 1) * D, h0:h0 + NH // 2, :]
                        a = Q_PART[blk]
                    sp.dma_start(dst, src[a]).then_inc(ld_stack[j], 16)

            store_stack(0)
            store_stack(1)
            load_gate_up(GU_RING)
            load_stack(0)
            store_stack(2)
            load_stack(1)
            load_gate_up(GU_RING + 1)
            load_stack(2)
            for n in range(GU_RING + 2, KF):
                load_gate_up(n)
            for j in range(3, 6):
                store_stack(j)
                if j > 3:
                    load_stack(j - 1)
            load_stack(5)
            for g in range(NG):
                sp.wait_ge(negmaxT_done, g + 1)
                for p in range(2):
                    sp.dma_start(q_stack[MAX_ROW + p:MAX_ROW + p + 1, g * R:(g + 1) * R, :],
                                 negmaxT[p * R:(p + 1) * R, g % 2, :]).then_inc(st_max[g], 16)
                if g == NG - EARLY - 1:
                    sp.wait_ge(h_done, len(FFN))
                    sp.dma_start(wo_sb[:, :, :], wo.rearrange("(k p) n -> p k n", p=P)).then_inc(ld_wo, 16)
                    sp.dma_start(acc[:, :, :], xT.rearrange("(k p) n -> p k n", p=P)).then_inc(ld_xT, 16)
            for i in range(B * KE):
                sp.wait_ge(y_done, i + 1)
                b, m = divmod(i, KE)
                sp.dma_start(yT[m * P:(m + 1) * P, toks(b)], out_sb[:, i % 2, :]).then_inc(st_y[i], 16)
            for i in range(B * KE):
                sp.wait_ge(st_y[i], 16)

        @block.gpsimd
        def _(pool):
            pool.memset(half[:, :], -0.5).then_inc(filled, 1)
            pool.wait_ge(filled, 1)
            pool.memset(v_ones[:, :, :, :, :], 1.0).then_inc(filled, 1)
            pool.wait_ge(filled, 2)
            for i in range(T // 2):
                pool.wait_ge(stat_done, 3 * (i + 1))
                pool.tensor_tensor(rstd[:, 2 * i:2 * i + 2], var_eps[:, 2 * i:2 * i + 2], half[:, :],
                                   ALU.pow).then_inc(rstd_done, 1)
                if i == 1:
                    pool.wait_ge(wqkv_hi, 1)
                    pool.wait_ge(ld_wqkv, 16)
                    pool.tensor_tensor(wqkv_l[:, :, :], wqkv_sb[:, :, :], wqkv_h[:, :, :].bitcast(F32),
                                       ALU.subtract).then_inc(wqkv_lo, 1)

            def gate_up_lo(n):
                pool.wait_ge(wgu_hi, n + 1)
                pool.wait_ge(ld_wgu[n % GU_RING], 16 * (n // GU_RING + 1))
                cols = slice(n * 2 * P, (n + 1) * 2 * P)
                pool.tensor_tensor(wgu_l[:, :, cols], wgu_sb[:, n % GU_RING, :, :],
                                   wgu_h[:, :, cols].bitcast(F32), ALU.subtract).then_inc(wgu_lo, 1)

            def hadamard_stage(s):
                src, dst = (wd_b, wd_a) if s % 2 else (wd_a, wd_b)
                if s:
                    pool.wait_ge(stage_done, 2 * s)
                else:
                    pool.wait_ge(had_out, 4)
                a = src[:, :, :].rearrange("p (u two w) n -> p two u (w n)", two=2, w=1 << s)
                o = dst[:, :, :].rearrange("p (u two w) n -> p two u (w n)", two=2, w=1 << s)
                pool.tensor_tensor(o[:, 0], a[:, 0], a[:, 1], ALU.add).then_inc(stage_done, 1)
                pool.tensor_tensor(o[:, 1], a[:, 0], a[:, 1], ALU.subtract).then_inc(stage_done, 1)

            for n in range(5):
                gate_up_lo(n)
            hadamard_stage(0)
            gate_up_lo(5)
            gate_up_lo(6)
            hadamard_stage(1)
            gate_up_lo(7)
            pool.wait_ge(wgu_lo, KF)
            pool.memset(k_stack[MAX_ROW:MAX_ROW + 2, :, :], 1.0).then_inc(filled, 1)
            pool.wait_ge(filled, 3)
            hadamard_stage(2)
            pool.wait_ge(w2_hi, 1)
            pool.tensor_tensor(w2_l[:, :, :], wd_b[:, :, :], w2_h[:, :, :].bitcast(F32),
                               ALU.subtract).then_inc(w2_lo, 1)

            for u in range(KF, len(FFN)):
                b, n = FFN[u]
                pool.wait_ge(h_done, KF)
                pool.wait_ge(silu_done, u + 1)
                pool.wait_ge(up_out, u - KF + 1)
                pool.tensor_tensor(h_sb[b][:, n, :], up[:, u % 2, :], silu[:, u % 2, :],
                                   ALU.mult).then_inc(h_done, 1)

            def split_h(i):
                pool.wait_ge(h_hi_done, i + 1)
                pool.tensor_tensor(h_lo[:, i, :], h_sb[0][:, i, :], h_hi[:, i, :].bitcast(F32),
                                   ALU.subtract).then_inc(h_lo_done, 1)

            for i in range(NG * NT):
                g, k = divmod(i, NT)
                pool.wait_ge(exp_done, i + 1)
                u = probs[:, g % 2, k, :]
                if k < 2:
                    v, pattern = u.rearrange("p (h q) -> p h q", h=2)[:, :, 0:P], [[0, 2], [1, P]]
                elif k < 4:
                    v = u.rearrange("p (h q) -> p h q", h=2)[:, :, 0:2 * P]
                    pattern = [[0, 2], [0, 2], [1, P]]
                else:
                    v, pattern = u.rearrange("p (h q) -> p h q", h=4)[:, :, 0:P], [[0, 4], [1, P]]
                pool.affine_select(out=v, in_=v, pattern=pattern, compare_op=ALU.is_ge, fill=0.0, base=0,
                                   channel_multiplier=-1).then_inc(probs_masked, 1)
                n = split_after(i - EARLY * NT)
                if n in range(POOL_SPLITS):
                    split_h(n)

        @block.scalar
        def _(act):
            act.dma_start(cst_sb[:, :, :], cst.rearrange("(c p) n -> p c n", p=P)).then_inc(ld_cst, 16)
            act.dma_start(vec_sb[:, :], vec).then_inc(ld_vec, 16)
            act.wait_ge(filled, 1)
            act.activation(table_warm[:, :], half[:, 0:1], ACT.Silu)
            act.wait_ge(ld_cst, 16)
            act.copy(ident_bf[:, :], ident).then_inc(consts_cast, 1)
            act.copy(mask_bf[:, :], cst_sb[:, 2, :]).then_inc(consts_cast, 1)

            def gate_up_hi(n):
                act.wait_ge(ld_wgu[n % GU_RING], 16 * (n // GU_RING + 1))
                act.copy(wgu_h[:, :, n * 2 * P:(n + 1) * 2 * P],
                         wgu_sb[:, n % GU_RING, :, :]).then_inc(wgu_hi, 1)

            def x_hi(b, k):
                act.wait_ge(xT_done, KE * b + k + 1)
                act.copy(xh[b][:, k, :], bank[:, TURN_BANK[b][k], :]).then_inc(xh_done, 1)

            def tile_hi(i):
                b, what = TILES[i]
                act.wait_ge(tile_done, i + 1)
                ps = bank[:, TILE_BANK[i], :]
                if what[0] == "f":
                    act.copy(fh[:, int(what[1]), toks(b)], ps).then_inc(tile_first, 1)
                    return
                j = STACKED.index(i)
                if what == "kv":
                    act.copy(vT[64:P, b, :], ps[64:P, :]).then_inc(vT_done, 1)
                    act.copy(part[0:64, j, 0, :], ps[0:64, :]).then_inc(tile_first, 1)
                else:
                    act.copy(part[:, j, 0, :], ps).then_inc(tile_first, 1)

            def mid_part(i):
                if TILES[i][1][0] == "f":
                    return
                j = STACKED.index(i)
                rows = slice(0, 64 if TILES[i][1] == "kv" else P)
                act.wait_ge(tile_rest, i + 1)
                act.copy(part[rows, j, 1, :], rest[rows, j % 2, :]).then_inc(part_m, 1)

            def gate(u):
                b, n = FFN[u]
                act.wait_ge(scales_ready, 3)
                act.wait_ge(gate_done, u + 1)
                if u >= 2:
                    act.wait_ge(h_done, u - 1)
                act.activation(silu[:, u % 2, :], bank[:, ffn_bank(u), :], ACT.Silu,
                               scale=s_gate[:, n:n + 1]).then_inc(silu_done, 1)
                if u == len(FFN) - 1:
                    act.activation(table_warm[:, :], half[:, 0:1], ACT.Exp)
                if b:
                    act.wait_ge(up_done, u + 1)
                    act.activation(up[:, u % 2, :], bank[:, ffn_bank(u) + 1, :], ACT.Copy,
                                   scale=s_up[:, n:n + 1]).then_inc(up_out, 1)

            last = None
            for kind, *at in OPENING:
                if kind == "T":
                    x_hi(at[0], 0)
                    x_hi(at[0], 1)
                    if at[0] == 0:
                        act.wait_ge(ld_wqkv, 16)
                        act.copy(wqkv_h[:, :, :], wqkv_sb[:, :, :]).then_inc(wqkv_hi, 1)
                    else:
                        gate_up_hi(0)
                        gate_up_hi(1)
                elif kind == "H":
                    for q in range(4):
                        act.wait_ge(had_made, q + 1)
                        act.copy(wd_a[:, 2 * q:2 * q + 2, :],
                                 bank[:, HAD_BANK[q], :].rearrange("p (k n) -> p k n", k=2)).then_inc(had_out, 1)
                elif kind == "F":
                    gate(at[0])
                elif kind != "V":
                    tile_hi(kind)
                    if last is not None:
                        mid_part(last)
                    last = kind
                    if kind in (4, 6):
                        gate_up_hi({4: 2, 6: 3}[kind])
                if kind == "F" and at[0] >= 2:
                    gate_up_hi(at[0] + 2)
            for u in range(AHEAD, len(FFN)):
                gate(u)
                if u + 2 < KF:
                    gate_up_hi(u + 2)
                if u == KF - 1:
                    act.wait_ge(stage_done, 6)
                    act.copy(w2_h[:, :, :], wd_b[:, :, :]).then_inc(w2_hi, 1)

            def exps(i):
                g, k = divmod(i, NT)
                act.wait_ge(t_done, i + 1)
                if g >= 2:
                    act.wait_ge(pv_done, C * (g - 2) + (1, 1, 3, 3, 4)[k])
                act.activation(probs[:, g % 2, k, :], bank[:, t_bank(i):t_bank(i) + 2, :], ACT.Exp,
                               scale=SCALE).then_inc(exp_done, 1)

            def split_h(i):
                b, n = divmod(i, KF)
                if i >= H_RING:
                    act.wait_ge(h_used, i - H_RING + 1)
                else:
                    act.wait_ge(h_done, len(FFN))
                act.copy(h_hi[:, i % H_RING, :], h_sb[b][:, n, :]).then_inc(h_hi_done, 1)

            act.wait_ge(wgu_lo, KF)
            for i in range(NG * NT):
                exps(i)
                slot = i - EARLY * NT
                if i == 9:
                    act.wait_ge(ld_wo, 16)
                    act.copy(wo_h[:, :, :], wo_sb[:, :, :]).then_inc(wo_hi, 1)
                if split_after(slot) is not None:
                    split_h(split_after(slot))

            def turned_hi(i):
                b, k = divmod(i, KE)
                act.wait_ge(ot_done, i + 1)
                act.copy(oh[:, k, toks(b)], bank[:, 4 + i, :]).then_inc(oh_done, 1)

            split_h(LAST_SPLIT + 1)
            turned_hi(0)
            turned_hi(1)
            for i in range(LAST_SPLIT + 2, B * KF):
                split_h(i)
            turned_hi(2)
            turned_hi(3)

        @block.vector
        def _(dve):
            def statistics(i):
                dve.wait_ge(ld_x[i], 16)
                for t in (2 * i, 2 * i + 1):
                    ins = dve.bn_stats(stats[:, t, :], x_sb[:, t, :])
                ins.then_inc(stat_done, 1)
                dve.wait_ge(stat_done, 3 * i + 1)
                for t in (2 * i, 2 * i + 1):
                    ins = dve.bn_aggr(mv[:, t, :], stats[:, t, :])
                ins.then_inc(stat_done, 1)
                dve.wait_ge(stat_done, 3 * i + 2)
                dve.tensor_scalar(var_eps[:, 2 * i:2 * i + 2], mv[:, 2 * i:2 * i + 2, 1], EPS, None,
                                  ALU.add).then_inc(stat_done, 1)

            def normalise(i):
                dve.wait_ge(rstd_done, i + 1)
                for t in (2 * i, 2 * i + 1):
                    dve.tensor_scalar(x_sb[:, t, :], x_sb[:, t, :], mv[:, t, 0:1], rstd[:, t:t + 1],
                                      ALU.subtract, ALU.mult).then_inc(norm_done, 1)

            def x_lo(b, k):
                dve.wait_ge(xh_done, KE * b + k + 1)
                dve.tensor_tensor(xl[b][:, k, :], bank[:, TURN_BANK[b][k], :], xh[b][:, k, :].bitcast(F32),
                                  ALU.subtract).then_inc(xl_done, 1)

            def tile_lo(i):
                b, what = TILES[i]
                dve.wait_ge(tile_first, i + 1)
                ps = bank[:, TILE_BANK[i], :]
                if what[0] == "f":
                    m = int(what[1])
                    dve.tensor_tensor(fl[:, m, toks(b)], ps, fh[:, m, toks(b)].bitcast(F32),
                                      ALU.subtract).then_inc(tile_rest, 1)
                    return
                j = STACKED.index(i)
                rows = slice(0, 64 if what == "kv" else P)
                if j >= 2:
                    dve.wait_ge(part_l, j - 1)
                dve.tensor_tensor(rest[rows, j % 2, :], ps[rows, :], part[rows, j, 0, :],
                                  ALU.subtract).then_inc(tile_rest, 1)

            def low_part(i):
                if TILES[i][1][0] == "f":
                    return
                j = STACKED.index(i)
                rows = slice(0, 64 if TILES[i][1] == "kv" else P)
                dve.wait_ge(part_m, j + 1)
                dve.tensor_tensor(part[rows, j, 2, :], rest[rows, j % 2, :], part[rows, j, 1, :],
                                  ALU.subtract).then_inc(part_l, 1)

            def v_out(b):
                dve.wait_ge(v_turned, b + 1)
                dve.wait_ge(filled, 2)
                dve.tensor_copy(v_ones[:, b, :, :, 0:D],
                                bank[:, V_BANK[b], 0:E].rearrange("p (c g d) -> p c g d", c=C, g=NKV)
                                ).then_inc(v_ready, 1)

            statistics(0)
            statistics(1)
            normalise(0)
            normalise(1)
            statistics(2)
            statistics(3)
            x_lo(0, 0)
            x_lo(0, 1)
            normalise(2)
            normalise(3)
            dve.wait_ge(ld_cst, 16)
            dve.wait_ge(ld_vec, 16)
            for k in range(KE):
                for m in range(KE):
                    dve.tensor_scalar(had[:, k, m * P:(m + 1) * P], cst_sb[:, 1, :], su_ug[:, k:k + 1],
                                      -1.0 if k and m else 1.0, ALU.mult, ALU.mult).then_inc(had_ready, 1)
            dve.tensor_scalar(s_gate[:, :], s_gate_raw, 1.0 / 16, None, ALU.mult).then_inc(scales_ready, 1)
            dve.scalar_tensor_tensor(s_up[:, :], s_up_raw, 1.0 / 16, su_dp, ALU.mult,
                                     ALU.mult).then_inc(scales_ready, 1)
            dve.tensor_scalar(s_dp[:, :], s_dp_raw, 1.0 / 32, None, ALU.mult).then_inc(scales_ready, 1)
            def gated(u):
                b, n = FFN[u]
                dve.wait_ge(up_done, u + 1)
                dve.wait_ge(silu_done, u + 1)
                dve.scalar_tensor_tensor(h_sb[b][:, n, :], bank[:, ffn_bank(u) + 1, :], s_up[:, n:n + 1],
                                         silu[:, u % 2, :], ALU.mult, ALU.mult).then_inc(h_done, 1)

            last = None
            for kind, *at in OPENING[1:]:
                if kind == "T":
                    x_lo(1, 0)
                    x_lo(1, 1)
                elif kind == "V":
                    v_out(at[0])
                elif kind == "F":
                    gated(at[0])
                elif kind != "H":
                    tile_lo(kind)
                    if last is not None:
                        low_part(last)
                    last = kind

            def unit_max(g, k):
                i = g * NS + k
                c, heads = S_UNITS[k]
                dve.wait_ge(s_done, i + 1)
                u = bank[:, 2 * (i % 2):2 * (i % 2) + 2, :]
                n = P * (c + 1)
                flat = u.rearrange("p u n -> p (u n)")
                if c < 2:
                    v = flat[:, 0:R * n].rearrange("p (h n) -> p h n", n=n)
                else:
                    v = u[:, :, 0:n]
                ins = dve.tensor_reduce(rowmax[:, g, c, heads[0]:heads[-1] + 1], v, AX.X, ALU.max)
                if k == MT_UNIT and g:
                    turned_max(g - 1, u[:, 1, :])
                    return
                ins.then_inc(max_done, 1)

            def turned_max(g, ps):
                if g >= 2:
                    dve.wait_ge(st_max[g - 2], 32)
                dve.tensor_copy(negmaxT[:, g % 2, :], ps.bitcast(BF16)[0:2 * R, 0:S]
                                ).then_inc(negmaxT_done, 1)
                dve.wait_ge(negmaxT_done, g + 1)
                dve.sem_inc(max_done, 1)

            def negated_max(g):
                dve.wait_ge(max_done, NS * (g + 1))
                dve.tensor_scalar(negmax[:, g, :, 0, :], rowmax[:, g, :, :], -1.0, None,
                                  ALU.mult).then_inc(negmax_done, 1)
                dve.wait_ge(negmax_done, 2 * g + 1)
                dve.scalar_tensor_tensor(negmax[:, g, :, 1, :], rowmax[:, g, :, :], -1.0,
                                         negmax[:, g, :, 0, :], ALU.mult, ALU.subtract
                                         ).then_inc(negmax_done, 1)

            for g in range(NG):
                for k in range(NS):
                    unit_max(g, k)
                    if k == 2 and 2 * g + AHEAD < KF:
                        gated(2 * g + AHEAD)
                negated_max(g)
                if 2 * g + AHEAD + 1 < KF:
                    gated(2 * g + AHEAD + 1)
            dve.wait_ge(s_done, NG * NS + 1)
            turned_max(NG - 1, bank[:, 1, :])

            def oT(g):
                dve.wait_ge(pv_done, C * (g + 1))
                dve.tensor_copy(oT_sb[:, g % 2, :], bank[:, 0, :]).then_inc(oT_out, 1)

            def normalised(g):
                b, kv = divmod(g, NKV)
                dve.wait_ge(o_turned, g + 1)
                v = bank[:, 1, :].rearrange("p (c r w) -> p c r w", c=C, r=R)
                dve.reciprocal(recip[:, :, :], v[:, :, :, D]).then_inc(recip_done, 1)
                dve.wait_ge(recip_done, g + 1)
                o = o_sb[:, b * C:(b + 1) * C, kv * R * D:(kv + 1) * R * D]
                dve.tensor_tensor(o.rearrange("p c (r d) -> p c r d", r=R), v[:, :, :, 0:D],
                                  recip[:, :, :].unsqueeze(3).to_broadcast([P, C, R, D]),
                                  ALU.mult).then_inc(o_done, 1)

            def split_h(i):
                b, n = divmod(i, KF)
                dve.wait_ge(h_hi_done, i + 1)
                if i == POOL_SPLITS:
                    dve.wait_ge(h_lo_done, i)
                dve.tensor_tensor(h_lo[:, i % H_RING, :], h_sb[b][:, n, :],
                                  h_hi[:, i % H_RING, :].bitcast(F32), ALU.subtract).then_inc(h_lo_done, 1)

            def add_ffn(b):
                dve.wait_ge(h_used, KF * (b + 1))
                dve.wait_ge(ld_xT, 16)
                for m in range(KE):
                    dve.scalar_tensor_tensor(acc[:, m, toks(b)], bank[:, 2 + m, :], s_dp[:, m:m + 1],
                                             acc[:, m, toks(b)], ALU.mult, ALU.add).then_inc(acc_done, 1)

            def turned_lo(i):
                b, k = divmod(i, KE)
                dve.wait_ge(oh_done, i + 1)
                dve.tensor_tensor(ol[:, k, toks(b)], bank[:, 4 + i, :], oh[:, k, toks(b)].bitcast(F32),
                                  ALU.subtract).then_inc(ol_done, 1)

            def result(i):
                b, m = divmod(i, KE)
                dve.wait_ge(attn_done, i + 1)
                dve.wait_ge(acc_done, i + 1)
                if i >= 2:
                    dve.wait_ge(st_y[i - 2], 16)
                dve.tensor_tensor(out_sb[:, i % 2, :], bank[:, 4 + i, :], acc[:, m, toks(b)],
                                  ALU.add).then_inc(y_done, 1)

            oT(0)
            dve.wait_ge(wo_hi, 1)
            dve.tensor_tensor(wo_l[:, :, :], wo_sb[:, :, :], wo_h[:, :, :].bitcast(F32),
                              ALU.subtract).then_inc(wo_lo, 1)
            for slot in range(SLOTS):
                g, k = divmod(slot + EARLY * NT, NT)
                if slot == 3:
                    normalised(0)
                if k == 3:
                    oT(g - 1)
                if slot == PAUSE - 1:
                    add_ffn(0)
                if k == 4:
                    normalised(g - 1)
                if (split_after(slot) or 0) >= POOL_SPLITS:
                    split_h(split_after(slot))
            split_h(LAST_SPLIT + 1)
            turned_lo(0)
            turned_lo(1)
            oT(NG - 1)
            split_h(LAST_SPLIT + 2)
            normalised(NG - 1)
            for i in range(LAST_SPLIT + 3, B * KF):
                split_h(i)
            turned_lo(2)
            turned_lo(3)
            result(0)
            result(1)
            add_ffn(1)
            result(2)
            result(3)

        @block.tensor
        def _(pe):
            def three_passes(out, wh, wl, vh, vl, lo_there=None):
                n = len(wh)
                for k in range(n):
                    pe.matmul(out, wh[k], vh[k], start=k == 0, stop=False)
                    pe.matmul(out, wl[k], vh[k], start=False, stop=False)
                if lo_there:
                    pe.wait_ge(*lo_there)
                for k in range(n):
                    ins = pe.matmul(out, wh[k], vl[k], start=False, stop=k == n - 1)
                return ins

            def turn_x(b):
                if b:
                    pe.wait_ge(had_out, 2)
                for pair in range(C // 2):
                    pe.wait_ge(norm_done, b * C + 2 * (pair + 1))
                    for k in range(KE):
                        for c in (2 * pair, 2 * pair + 1):
                            ins = pe.transpose(bank[:, TURN_BANK[b][k], c * P:(c + 1) * P],
                                               x_sb[:, b * C + c, k * P:(k + 1) * P], ident)
                        if pair == C // 2 - 1:
                            ins.then_inc(xT_done, 1)

            def projection(i):
                b, what = TILES[i]
                if i in (2, 3):
                    pe.wait_ge(had_out, i + 1)
                elif i == 5:
                    pe.wait_ge(v_ready, 1)
                elif i in (6, 7):
                    pe.wait_ge(xl_done, 2 * KE)
                elif i == 8:
                    pe.wait_ge(tile_rest, 5)
                elif i == 9:
                    pe.wait_ge(vT_done, 2)
                    pe.wait_ge(tile_rest, 6)
                ks = range(KE)
                pe.wait_ge(xh_done, KE * (b + 1))
                if what[0] == "f":
                    pe.wait_ge(had_ready, KE * KE)
                    pe.wait_ge(xl_done, KE * (b + 1))
                    m = slice(int(what[1]) * P, (int(what[1]) + 1) * P)
                    out = bank[:, TILE_BANK[i], :]
                    for k in ks:
                        pe.matmul(out, had[:, k, m], xh[b][:, k, :], start=k == 0, stop=False)
                        ins = pe.matmul(out, had[:, k, m], xl[b][:, k, :], start=False, stop=k == KE - 1)
                else:
                    pe.wait_ge(wqkv_lo, 1)
                    m = {"q0": 0, "q1": 1, "kv": 2}[what]
                    m = slice(m * P, (m + 1) * P)
                    ins = three_passes(bank[:, TILE_BANK[i], :], [wqkv_h[:, k, m] for k in ks],
                                       [wqkv_l[:, k, m] for k in ks], [xh[b][:, k, :] for k in ks],
                                       [xl[b][:, k, :] for k in ks], (xl_done, KE * (b + 1)))
                ins.then_inc(tile_done, 1)

            def turn_v(b):
                pe.wait_ge(vT_done, b + 1)
                pe.wait_ge(*((tile_rest, 7) if b else (xl_done, KE)))
                for c in range(C):
                    ins = pe.transpose(bank[:, V_BANK[b], c * 64:(c + 1) * 64],
                                       vT[64:P, b, c * P:(c + 1) * P], ident[64:P, 64:P])
                ins.then_inc(v_turned, 1)

            def gate_or_up(u, which):
                b, n = FFN[u]
                if which == 0:
                    pe.wait_ge(wgu_lo, n + 1)
                    pe.wait_ge(tile_rest, len(TILES) // B * (b + 1))
                    if u >= 2:
                        pe.wait_ge(silu_done, u - 1)
                elif u >= KF + 2:
                    pe.wait_ge(up_out, u - KF - 1)
                elif u >= 2:
                    pe.wait_ge(h_done, u - 1)
                m = slice((2 * n + which) * P, (2 * n + which + 1) * P)
                ks = range(KE)
                ins = three_passes(bank[:, ffn_bank(u) + which, :], [wgu_h[:, k, m] for k in ks],
                                   [wgu_l[:, k, m] for k in ks], [fh[:, k, toks(b)] for k in ks],
                                   [fl[:, k, toks(b)] for k in ks])
                ins.then_inc(up_done if which else gate_done, 1)

            def hadamard():
                pe.wait_ge(ld_wd, 16)
                for q in range(4):
                    for j in (2 * q, 2 * q + 1):
                        ins = pe.matmul(bank[:, HAD_BANK[q], (j % 2) * E:(j % 2 + 1) * E], cst_sb[:, 1, :],
                                        wd_b[:, j, :], start=True, stop=True)
                    ins.then_inc(had_made, 1)

            def turn_max(g, out):
                pe.wait_ge(negmax_done, 2 * (g + 1))
                for c in range(C):
                    ins = pe.transpose(out.bitcast(BF16)[0:2 * R, c * P:(c + 1) * P],
                                       negmax[:, g, c, :, :].rearrange("p a r -> p (a r)"), ident_bf[:, :])
                return ins

            def scores(g, k):
                b, kv = divmod(g, NKV)
                i = g * NS + k
                c, heads = S_UNITS[k]
                n = P * (c + 1)
                if i >= 2:
                    pe.wait_ge(max_done, i - 1)
                if k == 0:
                    pe.wait_ge(ld_stack[3 * b], 16 * TERMS)
                    pe.wait_ge(ld_stack[3 * b + 1 + kv // 2], 16 * TERMS)
                if k == MT_UNIT and g:
                    turn_max(g - 1, bank[:, 2 * (i % 2) + 1, :])
                u = bank[:, 2 * (i % 2):2 * (i % 2) + 2, :].rearrange("p u n -> p (u n)")
                for a, r in enumerate(heads):
                    at = a * (n if c < 2 else S)
                    pe.matmul(u[:, at:at + n], q_stack[0:MAX_ROW, g * R + r, c * P:(c + 1) * P],
                              k_stack[0:MAX_ROW, g, 0:n], start=True, stop=False)
                    ins = pe.matmul(u[:, at + n - P:at + n], ident_bf[:, :], mask_bf[:, :],
                                    start=False, stop=True)
                ins.then_inc(s_done, 1)

            def transposed_scores(g, k):
                i = g * NT + k
                if i >= 2:
                    pe.wait_ge(exp_done, i - 1)
                else:
                    pe.wait_ge(silu_done, len(FFN))
                    pe.wait_ge(up_out, KF)
                if k == 0:
                    pe.wait_ge(st_max[g], 32)
                    pe.wait_ge(filled, 3)
                u = bank[:, t_bank(i):t_bank(i) + 2, :].rearrange("p u n -> p (u n)")
                if k < 2:
                    blocks = [(2 * k + a, 0, a * S) for a in range(2)]
                elif k < 4:
                    blocks = [(2 * (k - 2) + a, j, a * S + at) for a in range(2) for j, at in ((3, 0), (1, P))]
                else:
                    blocks = [(a, 2, a * 2 * P) for a in range(R)]
                for r, j, at in blocks:
                    ins = pe.matmul(u[:, at:at + S - j * P], k_stack[0:STACK, g, j * P:(j + 1) * P],
                                    q_stack[0:STACK, g * R + r, j * P:S], start=True, stop=True)
                ins.then_inc(t_done, 1)

            def weighted_values(g, j):
                b, kv = divmod(g, NKV)
                pe.wait_ge(probs_masked, g * NT + {0: 2, 1: 4, 3: 4, 2: 5}[j])
                if j == 0 and g:
                    pe.wait_ge(oT_out, g)
                for r in range(R):
                    unit, at = {0: (r // 2, r % 2 * S), 1: (2 + r // 2, r % 2 * S + P),
                                3: (2 + r // 2, r % 2 * S), 2: (4, r * 2 * P)}[j]
                    ins = pe.matmul(bank[32 * r:32 * (r + 1), 0, j * P:S], v_ones[:, b, j, kv, :],
                                    probs[:, g % 2, unit, at:at + S - j * P], start=j == 0, stop=j == 2,
                                    skip_group_check=True)
                ins.then_inc(pv_done, 1)

            def turn_o(g):
                pe.wait_ge(oT_out, g + 1)
                if g:
                    pe.wait_ge(o_done, g)
                for c in range(C):
                    ins = pe.transpose(bank[:, 1, c * P:(c + 1) * P], oT_sb[:, g % 2, c * P:(c + 1) * P], ident)
                ins.then_inc(o_turned, 1)

            def down():
                for b in range(B):
                    if b:
                        pe.wait_ge(acc_done, KE * b)
                    for n in range(KF):
                        i = b * KF + n
                        pe.wait_ge(h_hi_done, i + 1)
                        pe.wait_ge(h_lo_done, i + 1)
                        hi, lo = h_hi[:, i % H_RING, :], h_lo[:, i % H_RING, :]
                        for m in range(KE):
                            out, ms = bank[:, 2 + m, :], slice(m * P, (m + 1) * P)
                            pe.matmul(out, w2_h[:, n, ms], hi, start=n == 0, stop=False)
                            yield
                            pe.matmul(out, w2_l[:, n, ms], hi, start=False, stop=False)
                            yield
                            ins = pe.matmul(out, w2_h[:, n, ms], lo, start=False, stop=n == KF - 1)
                            if m == KE - 1:
                                ins.then_inc(h_used, 1)
                            yield

            def turn_attention(b):
                pe.wait_ge(o_done, NKV * (b + 1))
                pe.wait_ge(exp_done, NG * NT - 1 + b)
                for k in range(KE):
                    for c in range(C):
                        ins = pe.transpose(bank[:, 4 + KE * b + k, c * P:(c + 1) * P],
                                           o_sb[:, b * C + c, k * P:(k + 1) * P], ident)
                    ins.then_inc(ot_done, 1)

            def project_out(b):
                pe.wait_ge(ol_done, KE * (b + 1))
                pe.wait_ge(wo_lo, 1)
                ks = range(KE)
                for m in range(KE):
                    ms = slice(m * P, (m + 1) * P)
                    three_passes(bank[:, 4 + KE * b + m, :], [wo_h[:, k, ms] for k in ks],
                                 [wo_l[:, k, ms] for k in ks], [oh[:, k, toks(b)] for k in ks],
                                 [ol[:, k, toks(b)] for k in ks]).then_inc(attn_done, 1)

            pe.wait_ge(ld_cst, 16)
            for kind, *at in OPENING:
                if kind == "T":
                    turn_x(at[0])
                elif kind == "H":
                    hadamard()
                elif kind == "V":
                    turn_v(at[0])
                elif kind == "F":
                    gate_or_up(at[0], 0)
                    gate_or_up(at[0], 1)
                else:
                    projection(kind)

            pe.wait_ge(consts_cast, 2)
            pe.wait_ge(v_ready, 2)
            pe.wait_ge(tile_rest, len(TILES))
            for g in range(NG):
                for k in range(NS):
                    scores(g, k)
                    u = 2 * g + AHEAD + k // 3
                    if u < len(FFN):
                        if k in (1, 2, 3, 5):
                            gate_or_up(u, k in (2, 5))
                    elif k < NT:
                        transposed_scores(g - (NG - EARLY), k)
            pe.wait_ge(max_done, NG * NS - 1)
            weighted_values(0, 0)
            weighted_values(0, 1)
            pe.wait_ge(max_done, NG * NS)
            turn_max(NG - 1, bank[:, 1, :]).then_inc(s_done, 1)
            weighted_values(0, 3)
            weighted_values(0, 2)

            steps = down()
            pe.wait_ge(w2_lo, 1)
            for slot in range(SLOTS):
                g, k = divmod(slot + EARLY * NT, NT)
                if slot == 3:
                    pe.wait_ge(negmaxT_done, NG)
                    turn_o(0)
                transposed_scores(g, k)
                if slot != PAUSE:
                    next(steps)
                    next(steps)
                if k == 0:
                    weighted_values(g - 1, 0)
                if k == 1:
                    weighted_values(g - 1, 1)
                if k == 2:
                    weighted_values(g - 1, 3)
                    weighted_values(g - 1, 2)
                if k == 4:
                    turn_o(g - 1)
            for _ in range(4):
                next(steps)
            turn_attention(0)
            for j in PV_ORDER:
                weighted_values(NG - 1, j)
            for _ in range(8):
                next(steps)
            turn_o(NG - 1)
            for _ in range(8):
                next(steps)
            turn_attention(1)
            project_out(0)
            for _ in steps:
                pass
            project_out(1)


def kernel(L0_attn_x, L0_attn_Wq, L0_attn_Wk, L0_attn_Wv, L0_attn_Wo, L0_ffn_SU_ug, L0_ffn_SU_dp,
           L0_ffn_Wscale_ug, L0_ffn_Wscale_dp, L0_ffn_W_up, L0_ffn_W_gate, L0_ffn_W_down):
    import numpy as np
    import concourse.bacc as bacc
    from concourse.bass_utils import run_bass_kernel_spmd

    def tiles(v):
        return np.asarray(v).reshape(-1, P).T

    x = np.ascontiguousarray(L0_attn_x).reshape(TOK, E)
    gate_up = np.stack([np.asarray(L0_ffn_W_gate).reshape(KF, P, E), np.asarray(L0_ffn_W_up).reshape(KF, P, E)], 1)
    wscale = np.asarray(L0_ffn_Wscale_ug)
    i = np.arange(P)
    hadamard = np.array([[1.0]], np.float32)
    while hadamard.shape[0] < P:
        hadamard = np.block([[hadamard, hadamard], [hadamard, -hadamard]])
    constants = np.concatenate([np.eye(P), hadamard, np.where(i[None, :] > i[:, None], MASKED, 0.0)], 0)
    arrays = {
        "x": x,
        "xT": x.T,
        "wqkv": np.concatenate([np.asarray(a) for a in (L0_attn_Wq, L0_attn_Wk, L0_attn_Wv)], 1),
        "wgu": gate_up.reshape(2 * F, E).T,
        "wd": np.asarray(L0_ffn_W_down).T,
        "wo": np.asarray(L0_attn_Wo),
        "vec": np.concatenate([tiles(L0_ffn_SU_ug), tiles(wscale[F:]), tiles(wscale[:F]), tiles(L0_ffn_SU_dp),
                               tiles(L0_ffn_Wscale_dp)], 1),
        "cst": constants.astype(np.float32),
    }
    arrays = {name: np.ascontiguousarray(a) for name, a in arrays.items()}
    nc = bacc.Bacc("TRN2", target_bir_lowering=False, num_devices=1)
    ins = [nc.dram_tensor(f"in_{name}", a.shape, mybir.dt.from_np(a.dtype), kind="ExternalInput").ap()
           for name, a in arrays.items()]
    out = nc.dram_tensor("out_yT", (E, TOK), F32, kind="ExternalOutput").ap()
    parts = nc.dram_tensor("parts", (6, P, 3, S), BF16, kind="Internal").ap()
    block_kernel(nc, *ins, out, parts)
    r = run_bass_kernel_spmd(nc, [{f"in_{name}": a for name, a in arrays.items()}], core_ids=[0])
    return np.ascontiguousarray(r.results[0]["out_yT"].T).reshape(B, S, E)
```

```python
from contextlib import ExitStack

import concourse.bass as bass
from concourse import mybir

ALU = mybir.AluOpType
ACT = mybir.ActivationFunctionType
AX = mybir.AxisListType
F32 = mybir.dt.float32
F32R = mybir.dt.float32r
BF16 = mybir.dt.bfloat16

P = 128
B, S, E = 2, 512, 256
TOK = B * S
NH, NKV = 16, 4
D = E // NH
R = NH // NKV
F = 1024
KE = E // P
KF = F // P
C = S // P
T = TOK // P
NG = B * NKV
EPS = 1e-5
SCALE = float(D) ** -0.5
MASKED = -1.0e30

Q_PART = (0, 0, 0, 1, 1, 2)
K_PART = (0, 1, 2, 0, 1, 0)
TERMS = len(Q_PART)
MAX_ROW = TERMS * D
STACK = MAX_ROW + 2
PV_ORDER = (0, 1, 3, 2)

TILES = [(b, what) for b in range(B) for what in ("kv", "q0", "q1", "f0", "f1")]
TILE_BANK = (4, 5, 6, 7, 1, 0, 2, 3, 1, 0)
STACKED = [i for i, (b, what) in enumerate(TILES) if what[0] != "f"]
TURN_BANK = ((0, 1), (2, 3))
V_BANK = (0, 2)
HAD_BANK = (4, 5, 6, 3)

OPENING = [("T", 0), (0,), (1,), ("V", 0), ("T", 1), (2,), (3,), (4,), (5,), ("H", 0), (6,), ("F", 0),
           ("F", 1), (7,), (8,), ("F", 2), (9,), ("V", 1), ("F", 3)]
PARTS_AFTER = {4: (1, 2), 6: (5,), 7: (6,), 8: (7,)}
AHEAD = sum(step[0] == "F" for step in OPENING)

S_UNITS = [(3, (0, 1)), (3, (2, 3)), (0, (0, 1, 2, 3)), (1, (0, 1, 2, 3)), (2, (0, 1)), (2, (2, 3))]
NS = len(S_UNITS)
MT_UNIT = 2
NT = 5
FFN = [(b, n) for b in range(B) for n in range(KF)]
EARLY = 2
WARM_UPS = 26
H_RING = 3
SLOTS = (NG - EARLY) * NT
DOWN_SLOTS = 3 * KF
GU_RING = 4

PIECES = [(0, 0, slice(0, S), 4), (0, 1, slice(0, S), 5), (1, 0, slice(0, S), 6),
          (1, 1, slice(0, S // 2), 7), (1, 1, slice(S // 2, S), 0)]


def ffn_bank(u):
    return 4 + 2 * (u % 2)


def t_bank(i):
    return 4 + 2 * (i % 2)


def split_after(slot):
    n, r = divmod(slot + 4, 3)
    return n if r == 0 and 0 <= n < KF + H_RING else None


def o_slot(slot):
    i, r = divmod(slot - NT - 3, 2 * NT)
    return i if r == 0 and i >= 0 else None


LAST_SPLIT = max(split_after(slot) or 0 for slot in range(SLOTS))
POOL_SPLITS = 2


def block_kernel(nc, x, xT, wqkv, wgu, wd, wo, vec, cst, yT, parts_dram, o_dram):
    with ExitStack() as ctx:
        def sb(name, shape, dt, c=ctx):
            return c.enter_context(nc.sbuf_tensor(name, shape, dt))

        def sem(name):
            return ctx.enter_context(nc.semaphore(name))

        q_stack = sb("q_stack", [P, B * NH, S], BF16)
        k_stack = sb("k_stack", [P, NG, S], BF16)
        v_ones = sb("v_ones", [P, B, C, NKV, 32], F32)
        cst_sb = sb("cst_sb", [P, 4, P], F32)
        ident = cst_sb[:, 0, :]
        ident_bf = sb("ident_bf", [P, P], BF16)
        mask_bf = sb("mask_bf", [P, P], BF16)
        had = sb("had", [P, KE, E], F32R)
        vec_sb = sb("vec_sb", [P, 28], F32)
        su_ug = vec_sb[:, 0:2]
        s_gate_raw, s_up_raw = vec_sb[:, 2:10], vec_sb[:, 10:18]
        su_dp, s_dp_raw = vec_sb[:, 18:26], vec_sb[:, 26:28]
        s_gate = sb("s_gate", [P, KF], F32)
        s_up = sb("s_up", [P, KF], F32)
        s_dp = sb("s_dp", [P, KE], F32)
        half = sb("half", [P, 2], F32)
        table_warm = sb("table_warm", [P, 1], F32)
        stats = sb("stats", [P, T, 6], F32)
        mv = sb("mv", [P, T, 2], F32)
        var_eps = sb("var_eps", [P, T], F32)
        rstd = sb("rstd", [P, T], F32)
        rowmax = sb("rowmax", [P, NG, C, R], F32)
        negmax = sb("negmax", [P, NG, C, 2, R], BF16)
        negmaxT = sb("negmaxT", [2 * R, 2, S], BF16)
        wd_b = sb("wd_b", [P, KF, E], F32)
        had128 = sb("had128", [P, P], F32R)

        with ExitStack() as c:
            xh = sb("xh", [P, KE, TOK // 2], F32R, c)
            xl = sb("xl", [P, KE, TOK // 2], F32R, c)
            xh1 = sb("xh1", [P, KE, TOK // 2], F32R, c)
            xl1 = sb("xl1", [P, KE, TOK // 2], F32R, c)
        xh, xl = [xh, xh1], [xl, xl1]
        h_b1 = sb("h_b1", [P, KF, S], F32)

        with ExitStack() as c:
            wd_h = sb("wd_h", [P, KF, E], F32R, c)
            wd_l = sb("wd_l", [P, KF, E], F32R, c)
        h_sb = [sb("h_b0", [P, KF, S], F32), h_b1]

        with ExitStack() as c:
            warm = sb("warm", [P, E], BF16, c)
        with ExitStack() as c:
            wd_a = sb("wd_a", [P, KF, E], F32, c)
        w2_h = sb("w2_h", [P, KF, E], F32R)

        with ExitStack() as c:
            x_sb = sb("x_sb", [P, T, E], F32, c)
        w2_l = sb("w2_l", [P, KF, E], F32R)

        with ExitStack() as c:
            part = sb("part", [P, len(STACKED), 3, S], BF16, c)
            rest = sb("rest", [P, 2, S], F32, c)
            vT = sb("vT", [P, B, S], F32, c)
            wqkv_sb = sb("wqkv_sb", [P, KE, 3 * P], F32, c)
            wqkv_h = sb("wqkv_h", [P, KE, 3 * P], F32R, c)
            wqkv_l = sb("wqkv_l", [P, KE, 3 * P], F32R, c)
            wgu_sb = sb("wgu_sb", [P, GU_RING, KE, 2 * P], F32, c)
            wgu_h = sb("wgu_h", [P, KE, 2 * F], F32R, c)
            wgu_l = sb("wgu_l", [P, KE, 2 * F], F32R, c)
            fh = sb("fh", [P, KE, TOK], F32R, c)
            fl = sb("fl", [P, KE, TOK], F32R, c)
            silu = sb("silu", [P, 2, S], F32, c)
            up = sb("up", [P, 2, S], F32, c)
        probs = sb("probs", [P, 2, NT, 2 * S], F32)
        acc = sb("acc", [P, KE, TOK], F32)
        num = sb("num", [P, 2, S], F32)
        den = sb("den", [P, 2, S], F32)
        with ExitStack() as c:
            oT_sb = sb("oT_sb", [P, 2, S], F32, c)
        out_sb = sb("out_sb", [P, 2, S], F32)
        h_hi = sb("h_hi", [P, H_RING, S], F32R)
        h_lo = sb("h_lo", [P, H_RING, S], F32R)
        oh = sb("oh", [P, KE, TOK], F32R)
        ol = sb("ol", [P, KE, TOK], F32R)
        wo_sb = sb("wo_sb", [P, KE, E], F32)
        wo_h = sb("wo_h", [P, KE, E], F32R)
        wo_l = sb("wo_l", [P, KE, E], F32R)

        bank = ctx.enter_context(nc.psum_tensor("bank", [P, 8, S], F32))

        ld_x = [sem(f"ld_x{i}") for i in range(4)]
        ld_cst, ld_vec, ld_wqkv, ld_wd = sem("ld_cst"), sem("ld_vec"), sem("ld_wqkv"), sem("ld_wd")
        ld_wgu = [sem(f"ld_wgu{i}") for i in range(GU_RING)]
        ld_wo, ld_xT = sem("ld_wo"), sem("ld_xT")
        st_parts = [sem(f"st_parts{j}") for j in range(len(STACKED))]
        ld_stack = [sem(f"ld_stack{j}") for j in range(len(STACKED))]
        st_max = [sem(f"st_max{g}") for g in range(NG)]
        st_y = [sem(f"st_y{i}") for i in range(len(PIECES))]
        consts_cast = sem("consts_cast")
        scales_ready = sem("scales_ready")
        had_ready = sem("had_ready")
        warm_there = sem("warm_there")
        filled = sem("filled")
        stat_done = sem("stat_done")
        rstd_done = sem("rstd_done")
        norm_done = sem("norm_done")
        xT_done = sem("xT_done")
        xh_done, xl_done = sem("xh_done"), sem("xl_done")
        wqkv_hi, wqkv_lo = sem("wqkv_hi"), sem("wqkv_lo")
        wgu_hi, wgu_lo = sem("wgu_hi"), sem("wgu_lo")
        tile_done = sem("tile_done")
        tile_first = sem("tile_first")
        tile_rest = sem("tile_rest")
        part_m, part_l = sem("part_m"), sem("part_l")
        vT_done = sem("vT_done")
        v_turned = sem("v_turned")
        v_ready = sem("v_ready")
        s_done = sem("s_done")
        max_done = sem("max_done")
        negmax_done = sem("negmax_done")
        negmaxT_done = sem("negmaxT_done")
        gate_done, up_done = sem("gate_done"), sem("up_done")
        silu_done, h_done = sem("silu_done"), sem("h_done")
        up_out = sem("up_out")
        stage_done = sem("stage_done")
        wd_hi, wd_lo = sem("wd_hi"), sem("wd_lo")
        had_made, had_out = sem("had_made"), sem("had_out")
        w2_hi, w2_lo = sem("w2_hi"), sem("w2_lo")
        h_hi_done, h_lo_done = sem("h_hi_done"), sem("h_lo_done")
        h_used = sem("h_used")
        t_done = sem("t_done")
        exp_done = sem("exp_done")
        probs_masked = sem("probs_masked")
        pv_done = sem("pv_done")
        oT_out = sem("oT_out")
        st_o = [sem(f"st_o{g}") for g in range(NG)]
        ld_den = [sem(f"ld_den{i}") for i in range(B * KE)]
        ld_num = [sem(f"ld_num{i}") for i in range(B * KE)]
        recip_done, o_done = sem("recip_done"), sem("o_done")
        acc_done = sem("acc_done")
        wo_hi, wo_lo = sem("wo_hi"), sem("wo_lo")
        oh_done, ol_done = sem("oh_done"), sem("ol_done")
        attn_done = sem("attn_done")
        y_done = sem("y_done")

        block = ctx.enter_context(nc.Block())

        def toks(b):
            return slice(b * S, (b + 1) * S)

        @block.sync
        def _(sp):
            x_t = x.rearrange("(t p) e -> p t e", p=P)
            for i in range(2):
                sp.dma_start(x_sb[:, 2 * i:2 * i + 2, :], x_t[:, 2 * i:2 * i + 2, :]).then_inc(ld_x[i], 16)
            sp.dma_start(wqkv_sb[:, :, :], wqkv.rearrange("(k p) n -> p k n", p=P)).then_inc(ld_wqkv, 16)
            for i in range(2, 4):
                sp.dma_start(x_sb[:, 2 * i:2 * i + 2, :], x_t[:, 2 * i:2 * i + 2, :]).then_inc(ld_x[i], 16)
            sp.dma_start(wd_b[:, :, :], wd.rearrange("(k p) n -> p k n", p=P)).then_inc(ld_wd, 16)
            wgu_t = wgu.rearrange("(k p) n -> p k n", p=P)

            def load_gate_up(n):
                if n >= GU_RING:
                    sp.wait_ge(wgu_hi, n - GU_RING + 1)
                    sp.wait_ge(wgu_lo, n - GU_RING + 1)
                sp.dma_start(wgu_sb[:, n % GU_RING, :, :],
                             wgu_t[:, :, n * 2 * P:(n + 1) * 2 * P]).then_inc(ld_wgu[n % GU_RING], 16)

            for n in range(GU_RING):
                load_gate_up(n)

            def store_stack(j):
                b, what = TILES[STACKED[j]]
                sp.wait_ge(tile_first, STACKED[j] + 1)
                sp.wait_ge(part_m, j + 1)
                sp.wait_ge(part_l, j + 1)
                rows = slice(0, 64 if what == "kv" else P)
                sp.dma_start(parts_dram[j, rows], part[rows, j, :, :]).then_inc(st_parts[j], 16)

            def load_stack(j):
                b, what = TILES[STACKED[j]]
                sp.wait_ge(st_parts[j], 16)
                rows = slice(0, 64 if what == "kv" else P)
                src = parts_dram[j, rows].rearrange("(h d) a t -> a d h t", d=D)
                for blk in range(TERMS):
                    if what == "kv":
                        dst = k_stack[blk * D:(blk + 1) * D, b * NKV:(b + 1) * NKV, :]
                        a = K_PART[blk]
                    else:
                        h0 = b * NH + int(what[1]) * NH // 2
                        dst = q_stack[blk * D:(blk + 1) * D, h0:h0 + NH // 2, :]
                        a = Q_PART[blk]
                    sp.dma_start(dst, src[a]).then_inc(ld_stack[j], 16)

            store_stack(0)
            store_stack(1)
            load_gate_up(GU_RING)
            load_stack(0)
            store_stack(2)
            load_stack(1)
            load_gate_up(GU_RING + 1)
            load_stack(2)
            for n in range(GU_RING + 2, KF):
                load_gate_up(n)
            for j in range(3, 6):
                store_stack(j)
                if j > 3:
                    load_stack(j - 1)
            load_stack(5)
            for g in range(NG):
                sp.wait_ge(negmaxT_done, g + 1)
                for p in range(2):
                    sp.dma_start(q_stack[MAX_ROW + p:MAX_ROW + p + 1, g * R:(g + 1) * R, :],
                                 negmaxT[p * R:(p + 1) * R, g % 2, :]).then_inc(st_max[g], 16)
                if g == NG - EARLY - 1:
                    sp.wait_ge(h_done, len(FFN))
                    sp.dma_start(wo_sb[:, :, :], wo.rearrange("(k p) n -> p k n", p=P)).then_inc(ld_wo, 16)
                    sp.dma_start(acc[:, :, :], xT.rearrange("(k p) n -> p k n", p=P)).then_inc(ld_xT, 16)
            for g in range(NG):
                sp.wait_ge(oT_out, g + 1)
                sp.dma_start(o_dram[g], oT_sb[:, g % 2, :]).then_inc(st_o[g], 16)
                if g % 2:
                    i = g // 2
                    sp.wait_ge(st_o[g - 1], 16)
                    sp.wait_ge(st_o[g], 16)
                    if i >= 2:
                        sp.wait_ge(ol_done, i - 1)
                    pair = o_dram[g - 1:g + 1].rearrange("g (r w d) t -> w (g r) d t", w=2, d=D)
                    sp.dma_start(den[:, i % 2, :], pair[1]).then_inc(ld_den[i], 16)
                    sp.dma_start(num[:, i % 2, :], pair[0]).then_inc(ld_num[i], 16)
            for i, (b, m, cols, _) in enumerate(PIECES):
                sp.wait_ge(y_done, i + 1)
                sp.dma_start(yT[m * P:(m + 1) * P, b * S + cols.start:b * S + cols.stop],
                             out_sb[:, m, cols]).then_inc(st_y[i], 16)
            for i in range(len(PIECES)):
                sp.wait_ge(st_y[i], 16)

        @block.gpsimd
        def _(pool):
            pool.memset(warm[:, :], 0.0).then_inc(warm_there, 1)
            pool.memset(half[:, :], -0.5).then_inc(filled, 1)
            pool.wait_ge(filled, 1)
            pool.memset(v_ones[:, :, :, :, :], 1.0).then_inc(filled, 1)
            pool.wait_ge(filled, 2)
            for i in range(T // 2):
                pool.wait_ge(stat_done, 3 * (i + 1))
                pool.tensor_tensor(rstd[:, 2 * i:2 * i + 2], var_eps[:, 2 * i:2 * i + 2], half[:, :],
                                   ALU.pow).then_inc(rstd_done, 1)
                if i == 1:
                    pool.wait_ge(wqkv_hi, 1)
                    pool.wait_ge(ld_wqkv, 16)
                    pool.tensor_tensor(wqkv_l[:, :, :], wqkv_sb[:, :, :], wqkv_h[:, :, :].bitcast(F32),
                                       ALU.subtract).then_inc(wqkv_lo, 1)

            def gate_up_lo(n):
                pool.wait_ge(wgu_hi, n + 1)
                pool.wait_ge(ld_wgu[n % GU_RING], 16 * (n // GU_RING + 1))
                cols = slice(n * 2 * P, (n + 1) * 2 * P)
                pool.tensor_tensor(wgu_l[:, :, cols], wgu_sb[:, n % GU_RING, :, :],
                                   wgu_h[:, :, cols].bitcast(F32), ALU.subtract).then_inc(wgu_lo, 1)

            def hadamard_stage(s):
                src, dst = (wd_b, wd_a) if s % 2 else (wd_a, wd_b)
                if s:
                    pool.wait_ge(stage_done, 2 * s)
                else:
                    pool.wait_ge(had_out, 4)
                a = src[:, :, :].rearrange("p (u two w) n -> p two u (w n)", two=2, w=1 << s)
                o = dst[:, :, :].rearrange("p (u two w) n -> p two u (w n)", two=2, w=1 << s)
                pool.tensor_tensor(o[:, 0], a[:, 0], a[:, 1], ALU.add).then_inc(stage_done, 1)
                pool.tensor_tensor(o[:, 1], a[:, 0], a[:, 1], ALU.subtract).then_inc(stage_done, 1)

            pool.wait_ge(ld_wd, 16)
            for i in range(2):
                ks = slice(i * KF // 2, (i + 1) * KF // 2)
                pool.wait_ge(wd_hi, i + 1)
                pool.tensor_tensor(wd_l[:, ks, :], wd_b[:, ks, :], wd_h[:, ks, :].bitcast(F32),
                                   ALU.subtract).then_inc(wd_lo, 1)
            for n in range(5):
                gate_up_lo(n)
            hadamard_stage(0)
            gate_up_lo(5)
            gate_up_lo(6)
            hadamard_stage(1)
            gate_up_lo(7)
            pool.wait_ge(wgu_lo, KF)
            pool.memset(k_stack[MAX_ROW:MAX_ROW + 2, :, :], 1.0).then_inc(filled, 1)
            pool.wait_ge(filled, 3)
            hadamard_stage(2)
            pool.wait_ge(w2_hi, 1)
            pool.tensor_tensor(w2_l[:, :, :], wd_b[:, :, :], w2_h[:, :, :].bitcast(F32),
                               ALU.subtract).then_inc(w2_lo, 1)

            for u in range(KF, len(FFN)):
                b, n = FFN[u]
                pool.wait_ge(h_done, KF)
                pool.wait_ge(silu_done, u + 1)
                pool.wait_ge(up_out, u - KF + 1)
                pool.tensor_tensor(h_sb[b][:, n, :], up[:, u % 2, :], silu[:, u % 2, :],
                                   ALU.mult).then_inc(h_done, 1)

            def split_h(i):
                b, n = divmod(i, KF)
                pool.wait_ge(h_hi_done, i + 1)
                if i > LAST_SPLIT:
                    pool.wait_ge(h_lo_done, i)
                pool.tensor_tensor(h_lo[:, i % H_RING, :], h_sb[b][:, n, :],
                                   h_hi[:, i % H_RING, :].bitcast(F32), ALU.subtract).then_inc(h_lo_done, 1)

            for i in range(NG * NT):
                g, k = divmod(i, NT)
                pool.wait_ge(exp_done, i + 1)
                u = probs[:, g % 2, k, :]
                if k < 2:
                    v, pattern = u.rearrange("p (h q) -> p h q", h=2)[:, :, 0:P], [[0, 2], [1, P]]
                elif k < 4:
                    v = u.rearrange("p (h q) -> p h q", h=2)[:, :, 0:2 * P]
                    pattern = [[0, 2], [0, 2], [1, P]]
                else:
                    v, pattern = u.rearrange("p (h q) -> p h q", h=4)[:, :, 0:P], [[0, 4], [1, P]]
                pool.affine_select(out=v, in_=v, pattern=pattern, compare_op=ALU.is_ge, fill=0.0, base=0,
                                   channel_multiplier=-1).then_inc(probs_masked, 1)
                n = split_after(i - EARLY * NT)
                if n in range(POOL_SPLITS):
                    split_h(n)
            for i in range(LAST_SPLIT + 1, B * KF):
                split_h(i)

        @block.scalar
        def _(act):
            act.dma_start(cst_sb[:, :, :], cst.rearrange("(c p) n -> p c n", p=P)).then_inc(ld_cst, 16)
            act.dma_start(vec_sb[:, :], vec).then_inc(ld_vec, 16)
            act.wait_ge(filled, 1)
            act.activation(table_warm[:, :], half[:, 0:1], ACT.Silu)
            act.wait_ge(ld_cst, 16)
            act.copy(ident_bf[:, :], ident).then_inc(consts_cast, 1)
            act.copy(mask_bf[:, :], cst_sb[:, 2, :]).then_inc(consts_cast, 1)
            act.copy(had128[:, :], cst_sb[:, 1, :]).then_inc(consts_cast, 1)
            act.wait_ge(ld_wqkv, 16)
            act.copy(wqkv_h[:, :, :], wqkv_sb[:, :, :]).then_inc(wqkv_hi, 1)
            act.wait_ge(ld_vec, 16)
            for k in range(KE):
                for m in range(KE):
                    act.activation(had[:, k, m * P:(m + 1) * P], cst_sb[:, 3 if k and m else 1, :], ACT.Copy,
                                   scale=su_ug[:, k:k + 1]).then_inc(had_ready, 1)

            def gate_up_hi(n):
                act.wait_ge(ld_wgu[n % GU_RING], 16 * (n // GU_RING + 1))
                act.copy(wgu_h[:, :, n * 2 * P:(n + 1) * 2 * P],
                         wgu_sb[:, n % GU_RING, :, :]).then_inc(wgu_hi, 1)

            def x_hi(b, k):
                act.wait_ge(xT_done, KE * b + k + 1)
                act.copy(xh[b][:, k, :], bank[:, TURN_BANK[b][k], :]).then_inc(xh_done, 1)

            def tile_hi(i):
                b, what = TILES[i]
                act.wait_ge(tile_done, i + 1)
                ps = bank[:, TILE_BANK[i], :]
                if what[0] == "f":
                    act.copy(fh[:, int(what[1]), toks(b)], ps).then_inc(tile_first, 1)
                    return
                j = STACKED.index(i)
                if what == "kv":
                    act.copy(vT[64:P, b, :], ps[64:P, :]).then_inc(vT_done, 1)
                    act.copy(part[0:64, j, 0, :], ps[0:64, :]).then_inc(tile_first, 1)
                else:
                    act.copy(part[:, j, 0, :], ps).then_inc(tile_first, 1)

            def gate(u):
                b, n = FFN[u]
                act.wait_ge(scales_ready, 3)
                act.wait_ge(gate_done, u + 1)
                if u >= 2:
                    act.wait_ge(h_done, u - 1)
                act.activation(silu[:, u % 2, :], bank[:, ffn_bank(u), :], ACT.Silu,
                               scale=s_gate[:, n:n + 1]).then_inc(silu_done, 1)
                if u == len(FFN) - 1:
                    act.activation(table_warm[:, :], half[:, 0:1], ACT.Exp)
                if b:
                    act.wait_ge(up_done, u + 1)
                    act.activation(up[:, u % 2, :], bank[:, ffn_bank(u) + 1, :], ACT.Copy,
                                   scale=s_up[:, n:n + 1]).then_inc(up_out, 1)

            for kind, *at in OPENING:
                if kind == "T":
                    x_hi(at[0], 0)
                    x_hi(at[0], 1)
                    if at[0]:
                        gate_up_hi(0)
                        gate_up_hi(1)
                elif kind == "H":
                    for q in range(4):
                        act.wait_ge(had_made, q + 1)
                        act.copy(wd_a[:, 2 * q:2 * q + 2, :],
                                 bank[:, HAD_BANK[q], :].rearrange("p (k n) -> p k n", k=2)).then_inc(had_out, 1)
                elif kind == "F":
                    gate(at[0])
                elif kind != "V":
                    tile_hi(kind)
                    if kind in (4, 6):
                        gate_up_hi({4: 2, 6: 3}[kind])
                if kind == "F" and at[0] >= 2:
                    gate_up_hi(at[0] + 2)
            for u in range(AHEAD, len(FFN)):
                gate(u)
                if u + 2 < KF:
                    gate_up_hi(u + 2)
                if u == KF - 1:
                    act.wait_ge(stage_done, 6)
                    act.copy(w2_h[:, :, :], wd_b[:, :, :]).then_inc(w2_hi, 1)

            def exps(i):
                g, k = divmod(i, NT)
                act.wait_ge(t_done, i + 1)
                if g >= 2:
                    act.wait_ge(pv_done, C * (g - 2) + (1, 1, 3, 3, 4)[k])
                act.activation(probs[:, g % 2, k, :], bank[:, t_bank(i):t_bank(i) + 2, :], ACT.Exp,
                               scale=SCALE).then_inc(exp_done, 1)

            def split_h(i):
                b, n = divmod(i, KF)
                if i >= H_RING:
                    act.wait_ge(h_used, i - H_RING + 1)
                else:
                    act.wait_ge(h_done, len(FFN))
                act.copy(h_hi[:, i % H_RING, :], h_sb[b][:, n, :]).then_inc(h_hi_done, 1)

            def attention_hi(i):
                b, k = divmod(i, KE)
                act.wait_ge(o_done, i + 1)
                act.copy(oh[:, k, toks(b)], num[:, i % 2, :]).then_inc(oh_done, 1)

            act.wait_ge(wgu_lo, KF)
            for i in range(NG * NT):
                exps(i)
                slot = i - EARLY * NT
                if i == EARLY * NT - 1:
                    act.wait_ge(ld_wo, 16)
                    act.copy(wo_h[:, :, :], wo_sb[:, :, :]).then_inc(wo_hi, 1)
                if split_after(slot) is not None:
                    split_h(split_after(slot))
                if o_slot(slot - 3) is not None:
                    attention_hi(o_slot(slot - 3))
            attention_hi(B * KE - 2)
            for i in range(LAST_SPLIT + 1, B * KF):
                split_h(i)
            attention_hi(B * KE - 1)

        @block.vector
        def _(dve):
            def statistics(i):
                dve.wait_ge(ld_x[i], 16)
                for t in (2 * i, 2 * i + 1):
                    ins = dve.bn_stats(stats[:, t, :], x_sb[:, t, :])
                ins.then_inc(stat_done, 1)
                dve.wait_ge(stat_done, 3 * i + 1)
                for t in (2 * i, 2 * i + 1):
                    ins = dve.bn_aggr(mv[:, t, :], stats[:, t, :])
                ins.then_inc(stat_done, 1)
                dve.wait_ge(stat_done, 3 * i + 2)
                dve.tensor_scalar(var_eps[:, 2 * i:2 * i + 2], mv[:, 2 * i:2 * i + 2, 1], EPS, None,
                                  ALU.add).then_inc(stat_done, 1)

            def normalise(i):
                dve.wait_ge(rstd_done, i + 1)
                for t in (2 * i, 2 * i + 1):
                    dve.tensor_scalar(x_sb[:, t, :], x_sb[:, t, :], mv[:, t, 0:1], rstd[:, t:t + 1],
                                      ALU.subtract, ALU.mult).then_inc(norm_done, 1)

            def x_lo(b, k):
                dve.wait_ge(xh_done, KE * b + k + 1)
                dve.tensor_tensor(xl[b][:, k, :], bank[:, TURN_BANK[b][k], :], xh[b][:, k, :].bitcast(F32),
                                  ALU.subtract).then_inc(xl_done, 1)

            def tile_lo(i):
                b, what = TILES[i]
                dve.wait_ge(tile_first, i + 1)
                ps = bank[:, TILE_BANK[i], :]
                if what[0] == "f":
                    m = int(what[1])
                    dve.tensor_tensor(fl[:, m, toks(b)], ps, fh[:, m, toks(b)].bitcast(F32),
                                      ALU.subtract).then_inc(tile_rest, 1)
                    return
                j = STACKED.index(i)
                rows = slice(0, 64 if what == "kv" else P)
                if j >= 2:
                    dve.wait_ge(part_l, j - 1)
                dve.tensor_tensor(rest[rows, j % 2, :], ps[rows, :], part[rows, j, 0, :],
                                  ALU.subtract).then_inc(tile_rest, 1)

            def mid_part(i):
                j = STACKED.index(i)
                rows = slice(0, 64 if TILES[i][1] == "kv" else P)
                dve.wait_ge(tile_rest, i + 1)
                dve.tensor_copy(part[rows, j, 1, :], rest[rows, j % 2, :]).then_inc(part_m, 1)

            def low_part(i):
                j = STACKED.index(i)
                rows = slice(0, 64 if TILES[i][1] == "kv" else P)
                dve.wait_ge(part_m, j + 1)
                dve.tensor_tensor(part[rows, j, 2, :], rest[rows, j % 2, :], part[rows, j, 1, :],
                                  ALU.subtract).then_inc(part_l, 1)

            def v_out(b):
                dve.wait_ge(v_turned, b + 1)
                dve.wait_ge(filled, 2)
                dve.tensor_copy(v_ones[:, b, :, :, 0:D],
                                bank[:, V_BANK[b], 0:E].rearrange("p (c g d) -> p c g d", c=C, g=NKV)
                                ).then_inc(v_ready, 1)

            statistics(0)
            statistics(1)
            normalise(0)
            normalise(1)
            statistics(2)
            x_lo(0, 0)
            x_lo(0, 1)
            statistics(3)
            normalise(2)
            normalise(3)

            def weights_hi(i):
                dve.wait_ge(ld_wd, 16)
                ks = slice(i * KF // 2, (i + 1) * KF // 2)
                dve.tensor_copy(wd_h[:, ks, :], wd_b[:, ks, :]).then_inc(wd_hi, 1)

            weights_hi(0)
            dve.wait_ge(ld_vec, 16)
            dve.tensor_scalar(s_gate[:, :], s_gate_raw, 1.0 / 16, None, ALU.mult).then_inc(scales_ready, 1)
            dve.scalar_tensor_tensor(s_up[:, :], s_up_raw, 1.0 / 16, su_dp, ALU.mult,
                                     ALU.mult).then_inc(scales_ready, 1)
            dve.tensor_scalar(s_dp[:, :], s_dp_raw, 1.0 / 32, None, ALU.mult).then_inc(scales_ready, 1)

            def gated(u):
                b, n = FFN[u]
                dve.wait_ge(up_done, u + 1)
                dve.wait_ge(silu_done, u + 1)
                dve.scalar_tensor_tensor(h_sb[b][:, n, :], bank[:, ffn_bank(u) + 1, :], s_up[:, n:n + 1],
                                         silu[:, u % 2, :], ALU.mult, ALU.mult).then_inc(h_done, 1)

            for kind, *at in OPENING[1:]:
                if kind == "T":
                    x_lo(1, 0)
                    x_lo(1, 1)
                    low_part(0)
                elif kind == "V":
                    v_out(at[0])
                elif kind == "F":
                    gated(at[0])
                elif kind != "H":
                    tile_lo(kind)
                    if kind == 1:
                        weights_hi(1)
                        mid_part(0)
                    for done in PARTS_AFTER.get(kind, ()):
                        mid_part(done)
                        low_part(done)

            def unit_max(g, k):
                i = g * NS + k
                c, heads = S_UNITS[k]
                dve.wait_ge(s_done, i + 1)
                u = bank[:, 2 * (i % 2):2 * (i % 2) + 2, :]
                n = P * (c + 1)
                flat = u.rearrange("p u n -> p (u n)")
                if c < 2:
                    v = flat[:, 0:R * n].rearrange("p (h n) -> p h n", n=n)
                else:
                    v = u[:, :, 0:n]
                ins = dve.tensor_reduce(rowmax[:, g, c, heads[0]:heads[-1] + 1], v, AX.X, ALU.max)
                if k == MT_UNIT and g:
                    turned_max(g - 1, u[:, 1, :])
                    return
                ins.then_inc(max_done, 1)

            def turned_max(g, ps):
                if g >= 2:
                    dve.wait_ge(st_max[g - 2], 32)
                dve.tensor_copy(negmaxT[:, g % 2, :], ps.bitcast(BF16)[0:2 * R, 0:S]
                                ).then_inc(negmaxT_done, 1)
                dve.wait_ge(negmaxT_done, g + 1)
                dve.sem_inc(max_done, 1)

            def negated_max(g):
                dve.wait_ge(max_done, NS * (g + 1))
                dve.tensor_scalar(negmax[:, g, :, 0, :], rowmax[:, g, :, :], -1.0, None,
                                  ALU.mult).then_inc(negmax_done, 1)
                dve.wait_ge(negmax_done, 2 * g + 1)
                dve.scalar_tensor_tensor(negmax[:, g, :, 1, :], rowmax[:, g, :, :], -1.0,
                                         negmax[:, g, :, 0, :], ALU.mult, ALU.subtract
                                         ).then_inc(negmax_done, 1)

            for g in range(NG):
                for k in range(NS):
                    unit_max(g, k)
                    if k == 2 and 2 * g + AHEAD < KF:
                        gated(2 * g + AHEAD)
                negated_max(g)
                if 2 * g + AHEAD + 1 < KF:
                    gated(2 * g + AHEAD + 1)
            dve.wait_ge(s_done, NG * NS + 1)
            turned_max(NG - 1, bank[:, 1, :])

            def oT(g):
                dve.wait_ge(pv_done, C * (g + 1))
                if g >= 2:
                    dve.wait_ge(st_o[g - 2], 16)
                dve.tensor_copy(oT_sb[:, g % 2, :], bank[:, g % 2, :]).then_inc(oT_out, 1)

            def divided(i):
                dve.wait_ge(ld_den[i], 16)
                dve.reciprocal(den[:, i % 2, :], den[:, i % 2, :]).then_inc(recip_done, 1)
                dve.wait_ge(recip_done, i + 1)
                dve.wait_ge(ld_num[i], 16)
                dve.tensor_tensor(num[:, i % 2, :], num[:, i % 2, :], den[:, i % 2, :],
                                  ALU.mult).then_inc(o_done, 1)

            def split_h(i):
                b, n = divmod(i, KF)
                dve.wait_ge(h_hi_done, i + 1)
                if i == POOL_SPLITS:
                    dve.wait_ge(h_lo_done, i)
                dve.tensor_tensor(h_lo[:, i % H_RING, :], h_sb[b][:, n, :],
                                  h_hi[:, i % H_RING, :].bitcast(F32), ALU.subtract).then_inc(h_lo_done, 1)

            def add_ffn(b):
                dve.wait_ge(h_used, KF * (b + 1))
                dve.wait_ge(ld_xT, 16)
                for m in range(KE):
                    dve.scalar_tensor_tensor(acc[:, m, toks(b)], bank[:, 2 + m, :], s_dp[:, m:m + 1],
                                             acc[:, m, toks(b)], ALU.mult, ALU.add).then_inc(acc_done, 1)

            def attention_lo(i):
                b, k = divmod(i, KE)
                dve.wait_ge(oh_done, i + 1)
                dve.tensor_tensor(ol[:, k, toks(b)], num[:, i % 2, :], oh[:, k, toks(b)].bitcast(F32),
                                  ALU.subtract).then_inc(ol_done, 1)

            def result(i):
                b, m, cols, at = PIECES[i]
                dve.wait_ge(attn_done, i + 1)
                dve.wait_ge(acc_done, KE * b + m + 1)
                dve.wait_ge(st_y[m] if b else st_o[NG - 2 + m], 16)
                dve.tensor_tensor(out_sb[:, m, cols], bank[:, at, cols],
                                  acc[:, m, b * S + cols.start:b * S + cols.stop], ALU.add).then_inc(y_done, 1)

            oT(0)
            dve.wait_ge(wo_hi, 1)
            dve.tensor_tensor(wo_l[:, :, :], wo_sb[:, :, :], wo_h[:, :, :].bitcast(F32),
                              ALU.subtract).then_inc(wo_lo, 1)
            for slot in range(SLOTS):
                g, k = divmod(slot + EARLY * NT, NT)
                if k == 3:
                    oT(g - 1)
                if slot == DOWN_SLOTS - 1:
                    add_ffn(0)
                if o_slot(slot) is not None:
                    divided(o_slot(slot))
                if o_slot(slot - 4) is not None:
                    attention_lo(o_slot(slot - 4))
                if (split_after(slot) or 0) >= POOL_SPLITS:
                    split_h(split_after(slot))
            oT(NG - 1)
            attention_lo(B * KE - 2)
            result(0)
            result(1)
            divided(B * KE - 1)
            attention_lo(B * KE - 1)
            add_ffn(1)
            for i in range(2, len(PIECES)):
                result(i)

        @block.tensor
        def _(pe):
            def three_passes(out, wh, wl, vh, vl, lo_there=None):
                n = len(wh)
                for k in range(n):
                    pe.matmul(out, wh[k], vh[k], start=k == 0, stop=False)
                    pe.matmul(out, wl[k], vh[k], start=False, stop=False)
                if lo_there:
                    pe.wait_ge(*lo_there)
                for k in range(n):
                    ins = pe.matmul(out, wh[k], vl[k], start=False, stop=k == n - 1)
                return ins

            def turn_x(b):
                for pair in range(C // 2):
                    pe.wait_ge(norm_done, b * C + 2 * (pair + 1))
                    for k in range(KE):
                        for c in (2 * pair, 2 * pair + 1):
                            ins = pe.transpose(bank[:, TURN_BANK[b][k], c * P:(c + 1) * P],
                                               x_sb[:, b * C + c, k * P:(k + 1) * P], ident)
                        if pair == C // 2 - 1:
                            ins.then_inc(xT_done, 1)

            def projection(i):
                b, what = TILES[i]
                if i == 5:
                    pe.wait_ge(v_ready, 1)
                elif i in (6, 7):
                    pe.wait_ge(xl_done, 2 * KE)
                elif i == 8:
                    pe.wait_ge(tile_rest, 5)
                elif i == 9:
                    pe.wait_ge(vT_done, 2)
                    pe.wait_ge(tile_rest, 6)
                ks = range(KE)
                pe.wait_ge(xh_done, KE * (b + 1))
                if what[0] == "f":
                    pe.wait_ge(had_ready, KE * KE)
                    pe.wait_ge(xl_done, KE * (b + 1))
                    m = slice(int(what[1]) * P, (int(what[1]) + 1) * P)
                    out = bank[:, TILE_BANK[i], :]
                    for k in ks:
                        pe.matmul(out, had[:, k, m], xh[b][:, k, :], start=k == 0, stop=False)
                        ins = pe.matmul(out, had[:, k, m], xl[b][:, k, :], start=False, stop=k == KE - 1)
                else:
                    pe.wait_ge(wqkv_lo, 1)
                    m = {"q0": 0, "q1": 1, "kv": 2}[what]
                    m = slice(m * P, (m + 1) * P)
                    ins = three_passes(bank[:, TILE_BANK[i], :], [wqkv_h[:, k, m] for k in ks],
                                       [wqkv_l[:, k, m] for k in ks], [xh[b][:, k, :] for k in ks],
                                       [xl[b][:, k, :] for k in ks], (xl_done, KE * (b + 1)))
                ins.then_inc(tile_done, 1)

            def turn_v(b):
                pe.wait_ge(vT_done, b + 1)
                pe.wait_ge(*((tile_rest, 7) if b else (xl_done, KE)))
                for c in range(C):
                    ins = pe.transpose(bank[:, V_BANK[b], c * 64:(c + 1) * 64],
                                       vT[64:P, b, c * P:(c + 1) * P], ident[64:P, 64:P])
                ins.then_inc(v_turned, 1)

            def gate_or_up(u, which):
                b, n = FFN[u]
                if which == 0:
                    pe.wait_ge(wgu_lo, n + 1)
                    pe.wait_ge(tile_rest, len(TILES) // B * (b + 1))
                    pe.wait_ge(had_out, 4)
                    if u >= 2:
                        pe.wait_ge(silu_done, u - 1)
                elif u >= KF + 2:
                    pe.wait_ge(up_out, u - KF - 1)
                elif u >= 2:
                    pe.wait_ge(h_done, u - 1)
                m = slice((2 * n + which) * P, (2 * n + which + 1) * P)
                ks = range(KE)
                ins = three_passes(bank[:, ffn_bank(u) + which, :], [wgu_h[:, k, m] for k in ks],
                                   [wgu_l[:, k, m] for k in ks], [fh[:, k, toks(b)] for k in ks],
                                   [fl[:, k, toks(b)] for k in ks])
                ins.then_inc(up_done if which else gate_done, 1)

            def hadamard():
                pe.wait_ge(consts_cast, 3)
                for q in range(4):
                    pe.wait_ge(wd_lo, q // 2 + 1)
                    pe.wait_ge(*((tile_rest, q + 1) if q < 3 else (xl_done, 2 * KE)))
                    out = bank[:, HAD_BANK[q], :]
                    pe.matmul(out, had128[:, :], wd_h[:, 2 * q:2 * q + 2, :], start=True, stop=False)
                    pe.matmul(out, had128[:, :], wd_l[:, 2 * q:2 * q + 2, :], start=False,
                              stop=True).then_inc(had_made, 1)

            def turn_max(g, out):
                pe.wait_ge(negmax_done, 2 * (g + 1))
                for c in range(C):
                    ins = pe.transpose(out.bitcast(BF16)[0:2 * R, c * P:(c + 1) * P],
                                       negmax[:, g, c, :, :].rearrange("p a r -> p (a r)"), ident_bf[:, :])
                return ins

            def scores(g, k):
                b, kv = divmod(g, NKV)
                i = g * NS + k
                c, heads = S_UNITS[k]
                n = P * (c + 1)
                if i >= 2:
                    pe.wait_ge(max_done, i - 1)
                if k == 0:
                    pe.wait_ge(ld_stack[3 * b], 16 * TERMS)
                    pe.wait_ge(ld_stack[3 * b + 1 + kv // 2], 16 * TERMS)
                if k == MT_UNIT and g:
                    turn_max(g - 1, bank[:, 2 * (i % 2) + 1, :])
                u = bank[:, 2 * (i % 2):2 * (i % 2) + 2, :].rearrange("p u n -> p (u n)")
                for a, r in enumerate(heads):
                    at = a * (n if c < 2 else S)
                    pe.matmul(u[:, at:at + n], q_stack[0:MAX_ROW, g * R + r, c * P:(c + 1) * P],
                              k_stack[0:MAX_ROW, g, 0:n], start=True, stop=False)
                    ins = pe.matmul(u[:, at + n - P:at + n], ident_bf[:, :], mask_bf[:, :],
                                    start=False, stop=True)
                ins.then_inc(s_done, 1)

            def transposed_scores(g, k):
                i = g * NT + k
                if i >= 2:
                    pe.wait_ge(exp_done, i - 1)
                else:
                    pe.wait_ge(silu_done, len(FFN))
                    pe.wait_ge(up_out, KF)
                if k == 0:
                    pe.wait_ge(st_max[g], 32)
                    pe.wait_ge(filled, 3)
                u = bank[:, t_bank(i):t_bank(i) + 2, :].rearrange("p u n -> p (u n)")
                if k < 2:
                    blocks = [(2 * k + a, 0, a * S) for a in range(2)]
                elif k < 4:
                    blocks = [(2 * (k - 2) + a, j, a * S + at) for a in range(2) for j, at in ((3, 0), (1, P))]
                else:
                    blocks = [(a, 2, a * 2 * P) for a in range(R)]
                for r, j, at in blocks:
                    ins = pe.matmul(u[:, at:at + S - j * P], k_stack[0:STACK, g, j * P:(j + 1) * P],
                                    q_stack[0:STACK, g * R + r, j * P:S], start=True, stop=True)
                ins.then_inc(t_done, 1)

            def weighted_values(g, j):
                b, kv = divmod(g, NKV)
                pe.wait_ge(probs_masked, g * NT + {0: 2, 1: 4, 3: 4, 2: 5}[j])
                if j == 0 and g >= 2:
                    pe.wait_ge(oT_out, g - 1)
                for r in range(R):
                    unit, at = {0: (r // 2, r % 2 * S), 1: (2 + r // 2, r % 2 * S + P),
                                3: (2 + r // 2, r % 2 * S), 2: (4, r * 2 * P)}[j]
                    ins = pe.matmul(bank[32 * r:32 * (r + 1), g % 2, j * P:S], v_ones[:, b, j, kv, :],
                                    probs[:, g % 2, unit, at:at + S - j * P], start=j == 0, stop=j == 2,
                                    skip_group_check=True)
                ins.then_inc(pv_done, 1)

            def down():
                for b in range(B):
                    if b:
                        pe.wait_ge(acc_done, KE * b)
                    for n in range(KF):
                        i = b * KF + n
                        pe.wait_ge(h_hi_done, i + 1)
                        pe.wait_ge(h_lo_done, i + 1)
                        hi, lo = h_hi[:, i % H_RING, :], h_lo[:, i % H_RING, :]
                        for m in range(KE):
                            out, ms = bank[:, 2 + m, :], slice(m * P, (m + 1) * P)
                            pe.matmul(out, w2_h[:, n, ms], hi, start=n == 0, stop=False)
                            yield
                            pe.matmul(out, w2_l[:, n, ms], hi, start=False, stop=False)
                            yield
                            ins = pe.matmul(out, w2_h[:, n, ms], lo, start=False, stop=n == KF - 1)
                            if m == KE - 1:
                                ins.then_inc(h_used, 1)
                            yield

            def project_out(b):
                pe.wait_ge(ol_done, KE * (b + 1))
                pe.wait_ge(exp_done, NG * NT - 1 + b)
                pe.wait_ge(oT_out, NG - 1)
                pe.wait_ge(wo_lo, 1)
                ks = range(KE)
                for of, m, cols, at in PIECES:
                    if of == b:
                        ms, ts = slice(m * P, (m + 1) * P), slice(b * S + cols.start, b * S + cols.stop)
                        three_passes(bank[:, at, cols], [wo_h[:, k, ms] for k in ks],
                                     [wo_l[:, k, ms] for k in ks], [oh[:, k, ts] for k in ks],
                                     [ol[:, k, ts] for k in ks]).then_inc(attn_done, 1)

            pe.wait_ge(warm_there, 1)
            for _ in range(WARM_UPS):
                pe.matmul(bank[:, 7, 0:E], warm[:, 0:P], warm[:, :], start=True, stop=True)

            pe.wait_ge(ld_cst, 16)
            for kind, *at in OPENING:
                if kind == "T":
                    turn_x(at[0])
                elif kind == "H":
                    hadamard()
                elif kind == "V":
                    turn_v(at[0])
                elif kind == "F":
                    gate_or_up(at[0], 0)
                    gate_or_up(at[0], 1)
                else:
                    projection(kind)

            pe.wait_ge(consts_cast, 3)
            pe.wait_ge(v_ready, 2)
            pe.wait_ge(tile_rest, len(TILES))
            for g in range(NG):
                for k in range(NS):
                    scores(g, k)
                    u = 2 * g + AHEAD + k // 3
                    if u < len(FFN):
                        if k in (1, 2, 3, 5):
                            gate_or_up(u, k in (2, 5))
                    elif k:
                        transposed_scores(g - (NG - EARLY), k - 1)
            pe.wait_ge(max_done, NG * NS - 1)
            weighted_values(0, 0)
            weighted_values(0, 1)
            pe.wait_ge(max_done, NG * NS)
            turn_max(NG - 1, bank[:, 1, :]).then_inc(s_done, 1)
            weighted_values(0, 3)
            weighted_values(0, 2)

            steps = down()
            pe.wait_ge(w2_lo, 1)
            for slot in range(SLOTS):
                g, k = divmod(slot + EARLY * NT, NT)
                transposed_scores(g, k)
                if slot < DOWN_SLOTS:
                    next(steps)
                    next(steps)
                if slot == 0:
                    pe.wait_ge(negmaxT_done, NG)
                if k == 0:
                    weighted_values(g - 1, 0)
                if k == 1:
                    weighted_values(g - 1, 1)
                if k == 2:
                    weighted_values(g - 1, 3)
                    weighted_values(g - 1, 2)
            next(steps)
            next(steps)
            for j in PV_ORDER[:-1]:
                weighted_values(NG - 1, j)
            next(steps)
            next(steps)
            weighted_values(NG - 1, PV_ORDER[-1])
            project_out(0)
            for _ in steps:
                pass
            project_out(1)


def kernel(L0_attn_x, L0_attn_Wq, L0_attn_Wk, L0_attn_Wv, L0_attn_Wo, L0_ffn_SU_ug, L0_ffn_SU_dp,
           L0_ffn_Wscale_ug, L0_ffn_Wscale_dp, L0_ffn_W_up, L0_ffn_W_gate, L0_ffn_W_down):
    import numpy as np
    import concourse.bacc as bacc
    from concourse.bass_utils import run_bass_kernel_spmd

    def tiles(v):
        return np.asarray(v).reshape(-1, P).T

    x = np.ascontiguousarray(L0_attn_x).reshape(TOK, E)
    gate_up = np.stack([np.asarray(L0_ffn_W_gate).reshape(KF, P, E), np.asarray(L0_ffn_W_up).reshape(KF, P, E)], 1)
    wscale = np.asarray(L0_ffn_Wscale_ug)
    i = np.arange(P)
    hadamard = np.array([[1.0]], np.float32)
    while hadamard.shape[0] < P:
        hadamard = np.block([[hadamard, hadamard], [hadamard, -hadamard]])
    constants = np.concatenate([np.eye(P), hadamard, np.where(i[None, :] > i[:, None], MASKED, 0.0), -hadamard], 0)
    arrays = {
        "x": x,
        "xT": x.T,
        "wqkv": np.concatenate([np.asarray(a) for a in (L0_attn_Wq, L0_attn_Wk, L0_attn_Wv)], 1),
        "wgu": gate_up.reshape(2 * F, E).T,
        "wd": np.asarray(L0_ffn_W_down).T,
        "wo": np.asarray(L0_attn_Wo),
        "vec": np.concatenate([tiles(L0_ffn_SU_ug), tiles(wscale[F:]), tiles(wscale[:F]), tiles(L0_ffn_SU_dp),
                               tiles(L0_ffn_Wscale_dp)], 1),
        "cst": constants.astype(np.float32),
    }
    arrays = {name: np.ascontiguousarray(a) for name, a in arrays.items()}
    nc = bacc.Bacc("TRN2", target_bir_lowering=False, num_devices=1)
    ins = [nc.dram_tensor(f"in_{name}", a.shape, mybir.dt.from_np(a.dtype), kind="ExternalInput").ap()
           for name, a in arrays.items()]
    out = nc.dram_tensor("out_yT", (E, TOK), F32, kind="ExternalOutput").ap()
    parts = nc.dram_tensor("parts", (6, P, 3, S), BF16, kind="Internal").ap()
    o_parts = nc.dram_tensor("o_parts", (NG, P, S), F32, kind="Internal").ap()
    block_kernel(nc, *ins, out, parts, o_parts)
    r = run_bass_kernel_spmd(nc, [{f"in_{name}": a for name, a in arrays.items()}], core_ids=[0])
    return np.ascontiguousarray(r.results[0]["out_yT"].T).reshape(B, S, E)
```
